# Optimizing a Trainium2 kernel written in Bass

```python
import numpy as np
import jax
import jax.numpy as jnp

def _softmax(x, axis=-1):
    return jax.nn.softmax(x, axis=axis)

def _gelu(x):
    return jax.nn.gelu(x, approximate=True)

def _silu(x):
    return jax.nn.silu(x)

def _sigmoid(x):
    return jax.nn.sigmoid(x)

def _layernorm(x, axis=-1, eps=1e-05):
    m = jnp.mean(x, axis=axis, keepdims=True)
    v = jnp.var(x, axis=axis, keepdims=True)
    return (x - m) / jnp.sqrt(v + eps)

def _scatter_add(tgt, idx, src, axis=0):
    return tgt.at[idx].add(src)

def _segment_sum(src, seg, n):
    return jax.ops.segment_sum(src, seg, n)
kernel_name = 'mk_xattn_seq_d1_seqx_r2_ba63a2'

def setup_inputs(seed: int=0):
    np.random.seed(seed)
    _w = jnp.asarray

    def _rec_inputs():
        import jax
        import jax.numpy as jnp
        _rk = jax.random.key(seed)
        x = -0.0003929 + 0.9999 * jax.random.normal(jax.random.fold_in(_rk, 1), (16, 512, 512), jnp.float32)
        _lenS = 512 - jax.random.randint(jax.random.fold_in(_rk, 7), (16,), 0, max(1, 512 // 4) + 1, jnp.int32)
        _lenS2 = 77 - jax.random.randint(jax.random.fold_in(_rk, 8), (16,), 0, max(1, 77 // 4) + 1, jnp.int32)
        _ctx_1024P = jax.random.normal(jax.random.fold_in(_rk, 11), (16, 16, 512), jnp.float32)
        _ctx_1024c = jax.random.dirichlet(jax.random.fold_in(_rk, 511), 0.3 * jnp.ones((16,), jnp.float32), (16, 77))
        _ctx_1024t = jnp.einsum('bsk,bkd->bsd', _ctx_1024c, _ctx_1024P)
        _ctx_1024t = _ctx_1024t * jax.lax.rsqrt(jnp.mean(jnp.square(_ctx_1024t)) + 1e-12) * 0.953939
        ctx_1024 = 2.81802e-05 + 1.00001 * (_ctx_1024t + 0.3 * jax.random.normal(jax.random.fold_in(_rk, 611), (16, 77, 512), jnp.float32))
        _validS = jnp.arange(512)[None, :] < _lenS[:, None]
        _validS2 = jnp.arange(77)[None, :] < _lenS2[:, None]
        _causal = jnp.tril(jnp.ones((512, 512), dtype=bool))
        mask_BxS_ff1 = jnp.where(jnp.ones((16, 512), dtype=bool), 1.0, 0.0).astype(jnp.float32)
        return (x, ctx_1024, mask_BxS_ff1)
    x, ctx_1024, mask_BxS_ff1 = _rec_inputs()

    def _L0_xattn_setup():
        import jax, jax.numpy as jnp
        import numpy as np
        B, L, D = (8, 1024, 512)
        key = jax.random.key(seed)
        ks = jax.random.split(key, 12)
        s = 1.0 / np.sqrt(D)
        return {'q': jax.random.normal(ks[0], (B, L, D), jnp.float32), 'k': jax.random.normal(ks[1], (B, L, D), jnp.float32), 'v': jax.random.normal(ks[2], (B, L, D), jnp.float32), 'mask': jnp.ones((B, L), jnp.float32), 'Wq': jax.random.normal(ks[3], (D, D), jnp.float32) * s, 'bq': jnp.zeros((D,), jnp.float32), 'Wk': jax.random.normal(ks[4], (D, D), jnp.float32) * s, 'bk': jnp.zeros((D,), jnp.float32), 'Wv': jax.random.normal(ks[5], (D, D), jnp.float32) * s, 'bv': jnp.zeros((D,), jnp.float32), 'Wg': jax.random.normal(ks[6], (2 * D, D), jnp.float32) * (1.0 / np.sqrt(2 * D)), 'bg': jnp.zeros((D,), jnp.float32)}
    _L0_xattn_all = _L0_xattn_setup()
    _L0_xattn_in = {k: v for k, v in _L0_xattn_all.items() if k in ('Wq', 'bq', 'Wk', 'bk', 'Wv', 'bv', 'Wg', 'bg')}
    del _L0_xattn_all
    return {'x': x, 'ctx_1024': ctx_1024, 'mask_BxS_ff1': mask_BxS_ff1, 'L0_xattn_Wq': _L0_xattn_in['Wq'], 'L0_xattn_bq': _L0_xattn_in['bq'], 'L0_xattn_Wk': _L0_xattn_in['Wk'], 'L0_xattn_bk': _L0_xattn_in['bk'], 'L0_xattn_Wv': _L0_xattn_in['Wv'], 'L0_xattn_bv': _L0_xattn_in['bv'], 'L0_xattn_Wg': _L0_xattn_in['Wg'], 'L0_xattn_bg': _L0_xattn_in['bg']}

def reference(x, ctx_1024, mask_BxS_ff1, L0_xattn_Wq, L0_xattn_bq, L0_xattn_Wk, L0_xattn_bk, L0_xattn_Wv, L0_xattn_bv, L0_xattn_Wg, L0_xattn_bg):
    import jax
    import jax.numpy as jnp

    def _L0_xattn_ref(q, k, v, mask, Wq, bq, Wk, bk, Wv, bv, Wg, bg):
        import jax, jax.numpy as jnp
        import numpy as np
        B, L, D = (8, 1024, 512)
        q0 = q
        qp = q @ Wq + bq
        kp = k @ Wk + bk
        vp = v @ Wv + bv
        scale = 1.0 / jnp.sqrt(jnp.asarray(qp.shape[-1], qp.dtype))
        w = jnp.einsum('bqd,bkd->bqk', qp, kp) * scale
        w = jax.nn.softmax(w, axis=-1)
        x = jnp.einsum('bqk,bkd->bqd', w, vp)
        gate = jnp.concatenate((qp, x), axis=-1) @ Wg + bg
        x = x * mask[..., None]
        x = x * jax.nn.sigmoid(gate)
        return x + q0
    x = _L0_xattn_ref(x, ctx_1024, ctx_1024, mask_BxS_ff1, L0_xattn_Wq, L0_xattn_bq, L0_xattn_Wk, L0_xattn_bk, L0_xattn_Wv, L0_xattn_bv, L0_xattn_Wg, L0_xattn_bg)
    return x

_drawn_inputs = setup_inputs


def setup_inputs(seed=0):
    import zlib

    import numpy as np

    out = dict(_drawn_inputs(seed))
    spreads = {'L0_xattn_bq': (0.0, 0.551),
     'L0_xattn_bk': (0.0, 0.8),
     'L0_xattn_bv': (0.0, 0.1),
     'L0_xattn_bg': (0.0, 0.654)}
    factors = {}
    for name, (base, spread) in spreads.items():
        noise = np.random.default_rng([zlib.crc32(name.encode()), seed]).standard_normal(out[name].shape)
        drawn = base * np.exp(spread * noise) if base else spread * noise
        out[name] = jnp.asarray(drawn.astype(out[name].dtype))
    for name, factor in factors.items():
        out[name] = (out[name] * factor).astype(out[name].dtype)
    return out
```

```python
from contextlib import ExitStack

import concourse.bass as bass
import concourse.mybir as mybir
from concourse.alu_op_type import AluOpType as ALU

F32 = mybir.dt.float32
F32R = mybir.dt.float32r
ACT = mybir.ActivationFunctionType
AX = mybir.AxisListType

P = 128
B, L, D = 16, 512, 512
S = 77
SP = S + 1
C = D // P
T = L // P
HI, LO = 0, 1
SCALE = float(D) ** -0.5

GB = 8
G = B // GB
GK = GB * SP
HB = GB // 2
HK = HB * SP
KT = -(-GK // P)
KROWS = [min(P, GK - k * P) for k in range(KT)]

LO_A = 45
LO_B = S - LO_A
K_A, K_B = S + LO_A, S + LO_B

NBANK = 4
J_VEC, J_WQT, J_BTOT, J_WQG = 0, 1, 1 + C, 2 + C
J_FIRST = 2 + 2 * C
H_FIRST = 2 * C
J_CTXT = 0
J_KPT = J_CTXT + 2 * C
J_SB = J_KPT + 2 * C
J_MT = J_SB + 2
J_V = J_MT + 2 * C


def v_steps():
    j, steps = J_V, []
    for k in range(KT + 1):
        step = {}
        if k >= 1:
            step["vt"] = (k - 1, j)
            j += 1
        if k < KT:
            step["v"] = (k, j)
            j += 1
        if k >= 1:
            step["vg"] = (k - 1, j)
            j += 1
        steps.append(step)
    return steps, j


V_STEPS, J_GROUP = v_steps()
V_JOB = {s["v"][0]: s["v"][1] for s in V_STEPS if "v" in s}
VT_JOB = {s["vt"][0]: s["vt"][1] for s in V_STEPS if "vt" in s}
H_CTXT, H_KPT, H_VT = 0, 2 * C, 4 * C
H_GROUP = 4 * C + KT
J_ALL = J_FIRST + G * J_GROUP

PRODUCTS = [(HI, HI), (HI, LO), (LO, HI)]


def build(nc, x, ctx_in, mask, wq, bq, wk, bk, wv, bv, wg, bg, out):
    with ExitStack() as es:
        def sb(name, shape, dt=F32):
            return es.enter_context(nc.sbuf_tensor(name, shape, dt))

        def sem(name):
            return es.enter_context(nc.semaphore(name))

        bank = [es.enter_context(nc.psum_tensor(f"bank{i}", [P, 512], F32)) for i in range(8)]
        gate_ps, attn_ps, turn_ps = bank[0:2], bank[2:4], bank[4:6]
        score_ps, turn_a_ps = bank[6], bank[7]
        turn_b_ps = score_ps

        v_dram = nc.dram_tensor("v_scratch", [B * SP, 2, 2 * D], F32, kind="Internal").ap()

        W_HL = 2 * C * D
        XT_WORDS = 2 * C * L
        arena_r = sb("arena_r", [P, 2 * 2 * C * GK + 4 * W_HL + 2 * D + 2 * 2 * D], F32R)
        at = [0]

        def take(words):
            at[0] += words
            return arena_r[:, at[0] - words:at[0]]

        ctxT_w, kpT_w = take(2 * C * GK), take(2 * C * GK)
        wqT_w, wk_w, wv_w, wg2_w = take(W_HL), take(W_HL), take(W_HL), take(W_HL)
        vT = take(2 * D).rearrange("p (s c k) -> p s c k", s=2, c=C)
        v_st = take(2 * 2 * D).rearrange("p (s n) -> p s n", s=2)
        ctxT = ctxT_w.rearrange("p (s c b k) -> p s c b k", s=2, c=C, b=GB)
        kpT = kpT_w.rearrange("p (s c b k) -> p s c b k", s=2, c=C, b=GB)
        wg1_s = kpT_w[:, 0:W_HL].rearrange("p (s c n) -> p s c n", s=2, c=C)
        wqT, wk_s, wv_s, wg2_s = (w.rearrange("p (s c n) -> p s c n", s=2, c=C) for w in (wqT_w, wk_w, wv_w, wg2_w))
        wqg = sb("wqg", [P, 2, C, D], F32R)
        bq_bc = sb("bq_bc", [P, 2, C, P], F32R)
        row0 = sb("row0", [P, P], F32R)
        xT = [w[:, 0:XT_WORDS].rearrange("p (s c q) -> p s c q", s=2, c=C) for w in (ctxT_w, kpT_w)]
        v_ext = [wqT_w[:, i * 4 * D:(i + 1) * 4 * D].rearrange("p (h n) -> p h n", h=2) for i in range(2)]
        MB = 5 * SP
        mt_b = [wk_w[:, i * 2 * MB:(i + 1) * 2 * MB].rearrange("p (s c k) -> p s c k", s=2, c=C + 1) for i in range(2)]
        wT = wk_w[:, 4 * MB:4 * MB + 2 * L].rearrange("p (h q) -> p h q", h=2)

        rows_w = sb("rows_w", [P, 2, C * D])
        stage = [rows_w[:, i, :].rearrange("p (c n) -> p c n", c=C) for i in range(2)]
        x_rows = [rows_w[:, i, :].rearrange("p (t n) -> p t n", t=T) for i in range(2)]
        work = sb("work", [P, GB * D])
        ctx_rows = work[:, :].rearrange("p (b n) -> p b n", b=GB)
        out_sb = work[:, 0:T * D].rearrange("p (t n) -> p t n", t=T)
        tanh_sb = work[:, T * D:(T + 2) * D].rearrange("p (i n) -> p i n", i=2)
        prod_sb = work[:, (T + 2) * D:(T + 4) * D].rearrange("p (i n) -> p i n", i=2)
        mt = sb("mt", [P, B, C + 1, SP])
        small = sb("small", [P, 4 * D])
        v_f, vg_f, bv_bc, btot = (small[:, i * D:(i + 1) * D] for i in range(4))
        o = 0
        soft = []
        for n in (T * S, T * S, T * S, T * K_A, T * K_B):
            soft.append(small[:, o:o + n].rearrange("p (t k) -> p t k", t=T))
            o += n
        shifted, expd, prob, w_a, w_b = soft
        stat = sb("stat", [P, 3, T])
        rowmax, rowsum, rinv = stat[:, 0, :], stat[:, 1, :], stat[:, 2, :]
        ident = sb("ident", [P, P])
        ones = sb("ones", [P, P])
        vec_rows = sb("vec_rows", [B * T + 2 * C, P])
        vec = sb("vec", [P, B * T + 2 * C])
        bq_c, bk_c = vec[:, B * T:B * T + C], vec[:, B * T + C:B * T + 2 * C]
        half_mask = sb("half_mask", [P, B * T])

        wq_in, wg1_in, wk_in, wv_in, wg2_in = (sem(n) for n in ("wq_in", "wg1_in", "wk_in", "wv_in", "wg2_in"))
        vec_in, bias_in, ctx_in_s = sem("vec_in"), sem("bias_in"), sem("ctx_in_s")
        ones_made, ident_zeroed, ident_made, row0_made = (sem(n) for n in ("ones_made", "ident_zeroed", "ident_made", "row0_made"))
        vec_made, bq_made, pads_made = sem("vec_made"), sem("bq_made"), sem("pads_made")
        job_done = sem("job_done")
        hi_made = sem("hi_made")
        job_drained = sem("job_drained")
        wg1_hi, wg1_split = sem("wg1_hi"), sem("wg1_split")
        w_hi, w_split = sem("w_hi"), sem("w_split")
        v_hi, v_lo, vg_hi, vg_lo = sem("v_hi"), sem("v_lo"), sem("vg_hi"), sem("vg_lo")
        v_stored, vg_stored = sem("v_stored"), sem("vg_stored")
        x_in = [[sem(f"x_in{i}{t}") for t in range(T)] for i in range(2)]
        vext_in = [sem(f"vext_in{i}") for i in range(2)]
        mt_split_hi, mt_split = sem("mt_split_hi"), sem("mt_split")
        x_turned, xT_hi, xT_made = sem("x_turned"), sem("xT_hi"), sem("xT_made")
        scores_done = sem("scores_done")
        max_made, shift_made, exp_made = sem("max_made"), sem("shift_made"), sem("exp_made")
        sum_made, rinv_made, prob_made = sem("sum_made"), sem("rinv_made"), sem("prob_made")
        prob_hi, prob_split = sem("prob_hi"), sem("prob_split")
        prob_stacked_a, prob_stacked_b = sem("prob_stacked_a"), sem("prob_stacked_b")
        wa_turned, wb_turned, wTa_made, wTb_made = sem("wa_turned"), sem("wb_turned"), sem("wTa_made"), sem("wTb_made")
        gate_done, attn_done = sem("gate_done"), sem("attn_done")
        tanh_made, prod_made, out_made = sem("tanh_made"), sem("prod_made"), sem("out_made")
        stored = [sem(f"stored{t}") for t in range(T)]

        x_v = x.rearrange("b (t p) d -> b t p d", p=P)
        out_v = out.rearrange("b (t p) d -> b t p d", p=P)

        def w_rows(w):
            return w.rearrange("(c p) n -> p c n", p=P)

        def f32(ap):
            return ap.bitcast(F32)

        def past(eng, sem_, value):
            if not isinstance(value, int) or value > 0:
                eng.wait_ge(sem_, value)

        block = es.enter_context(nc.Block())

        @block.sync
        def _(sync):
            sync.dma_start(stage[0], w_rows(wq)).then_inc(wq_in, 16)
            sync.dma_start(vec_rows[0:B * T, :], mask.rearrange("b (t p) -> (b t) p", p=P)).then_inc(vec_in, 16)
            sync.dma_start(vec_rows[B * T:B * T + C, :], bq.rearrange("(c p) -> c p", p=P)).then_inc(vec_in, 16)
            sync.dma_start(vec_rows[B * T + C:B * T + 2 * C, :], bk.rearrange("(c p) -> c p", p=P)).then_inc(vec_in, 16)
            sync.dma_start(stage[1], w_rows(wg[0:D, :])).then_inc(wg1_in, 16)
            sync.dma_start(btot, bg.rearrange("(a n) -> a n", a=1).broadcast_to([P, D])).then_inc(bias_in, 16)
            sync.dma_start(bv_bc, bv.rearrange("(a n) -> a n", a=1).broadcast_to([P, D])).then_inc(bias_in, 16)
            sync.dma_start(ctx_rows[0:S], ctx_in[0:GB].rearrange("b k d -> k b d")).then_inc(ctx_in_s, 16)
            sync.wait_ge(job_done, J_WQT + C)
            sync.dma_start(stage[0], w_rows(wk)).then_inc(wk_in, 16)
            sync.wait_ge(wg1_split, 1)
            sync.dma_start(stage[1], w_rows(wv)).then_inc(wv_in, 16)
            sync.wait_ge(w_split, 1)
            sync.dma_start(stage[0], w_rows(wg[D:2 * D, :])).then_inc(wg2_in, 16)
            for g in range(G):
                if g + 1 < G:
                    sync.wait_ge(job_done, J_FIRST + g * J_GROUP + J_KPT)
                    sync.dma_start(ctx_rows[0:S], ctx_in[(g + 1) * GB:(g + 2) * GB].rearrange("b k d -> k b d")).then_inc(ctx_in_s, 16)
                for step in V_STEPS:
                    for what, made, done, cols in (("v", v_lo, v_stored, 0), ("vg", vg_lo, vg_stored, D)):
                        if what in step:
                            k = step[what][0]
                            r0 = g * GK + k * P
                            sync.wait_ge(made, g * KT + k + 1)
                            sync.dma_start(v_dram[r0:r0 + KROWS[k], :, cols:cols + D],
                                           f32(v_st[0:KROWS[k], :, cols:cols + D])).then_inc(done, 16)
                    if g == 0 and step is V_STEPS[1]:
                        sync.wait_ge(w_split, 3)
                        for b in range(2):
                            for t in range(T):
                                sync.dma_start(x_rows[b][:, t, :], x_v[b, t]).then_inc(x_in[b][t], 16)

            def load_vext(b, i):
                r = b * SP
                for h, lo0, n in ((0, 0, LO_A), (1, LO_A, LO_B)):
                    sync.dma_start(f32(v_ext[i][0:S, h, :]), v_dram[bass.ds(r, S), HI, :]).then_inc(vext_in[i], 16)
                    sync.dma_start(f32(v_ext[i][S:S + n, h, :]), v_dram[bass.ds(r + lo0, n), LO, :]).then_inc(vext_in[i], 16)

            sync.wait_ge(v_stored, 16 * G * KT)
            sync.wait_ge(vg_stored, 16 * G * KT)
            sync.wait_ge(job_done, J_ALL)
            for b in range(2):
                load_vext(b, b)

            def batch(b, i, more):
                for t in range(T):
                    sync.wait_ge(out_made, b * T + (t + 1))
                    sync.dma_start(out_v[b, t], out_sb[:, t, :]).then_inc(stored[t], 16)
                    if more:
                        sync.dma_start(x_rows[i][:, t, :], x_v[b + 2, t]).then_inc(x_in[i][t], 16)
                if more:
                    sync.wait_ge(attn_done, b * T + T)
                    load_vext(b + 2, i)

            for i in range(2):
                batch(i, i, True)
            with sync.Fori(1, B // 2 - 1) as j:
                for i in range(2):
                    batch(2 * j + i, i, True)
            for i in range(2):
                batch(B - 2 + i, i, False)
            for t in range(T):
                sync.wait_ge(stored[t], 16 * B)

        @block.tensor
        def _(pe):
            def products(ps, lhs, rhs, sem_, inc=1):
                n, last = 0, None
                for c in range(C):
                    for s, m in PRODUCTS:
                        last = pe.matmul(ps, lhs(s, c), rhs(m, c), start=(n == 0), stop=(n == 3 * C - 1))
                        n += 1
                if sem_ is not None:
                    last.then_inc(sem_, inc)

            pe.wait_ge(ident_made, 1)
            pe.wait_ge(vec_in, 48)
            NV = B * T + 2 * C
            pe.transpose(bank[J_VEC][:, 0:NV], vec_rows[:, :], ident[0:NV, 0:NV]).then_inc(job_done, 1)
            pe.wait_ge(wq_in, 16)
            for ec in range(C):
                j = J_WQT + ec
                if j >= NBANK:
                    pe.wait_ge(job_drained, j - NBANK + 1)
                for dc in range(C):
                    last = pe.transpose(bank[j % NBANK][:, dc * P:(dc + 1) * P], stage[0][:, dc, ec * P:(ec + 1) * P], ident[:, :])
                last.then_inc(job_done, 1)
            pe.wait_ge(wg1_split, 1)
            pe.wait_ge(bq_made, 1)
            pe.wait_ge(job_drained, J_BTOT - NBANK + 1)
            products(bank[J_BTOT % NBANK][:, :], lambda s, c: bq_bc[:, s, c, :], lambda s, c: wg1_s[:, s, c, :], job_done)
            for dc in range(C):
                j = J_WQG + dc
                pe.wait_ge(job_drained, max(J_WQT + C, j - NBANK + 1))
                products(bank[j % NBANK][:, :], lambda s, c: wqT[:, s, c, dc * P:(dc + 1) * P],
                         lambda s, c: wg1_s[:, s, c, :], job_done)

            with pe.Fori(0, G) as g:
                base = g * J_GROUP + J_FIRST

                def bank_free(j):
                    pe.wait_ge(job_drained, base + max(j - NBANK + 1, 0))
                    return bank[j % NBANK]

                pe.wait_ge(ctx_in_s, g * 16 + 16)
                for c in range(C):
                    for h in range(2):
                        j = J_CTXT + 2 * c + h
                        ps = bank_free(j)[:, 0:HK].rearrange("p (b k) -> p b k", b=HB)
                        for i in range(HB):
                            last = pe.transpose(ps[:, i, 0:S], ctx_rows[0:S, h * HB + i, c * P:(c + 1) * P], ident[0:S, 0:S])
                        last.then_inc(job_done, 1)
                pe.wait_ge(w_split, 1)
                pe.wait_ge(job_drained, base + J_KPT)
                for ec in range(C):
                    for h in range(2):
                        ps = bank_free(J_KPT + 2 * ec + h)[:, 0:HK]
                        products(ps, lambda s, c: wk_s[:, s, c, ec * P:(ec + 1) * P],
                                 lambda s, c: ctxT[:, s, c, h * HB:(h + 1) * HB, :], job_done)
                pe.wait_ge(job_drained, base + J_SB)
                for h in range(2):
                    ps = bank_free(J_SB + h)[:, 0:HK]
                    products(ps, lambda s, c: bq_bc[:, s, c, :], lambda s, c: kpT[:, s, c, h * HB:(h + 1) * HB, :], job_done)
                for dc in range(C):
                    for h in range(2):
                        ps = bank_free(J_MT + 2 * dc + h)[:, 0:HK]
                        products(ps, lambda s, c: wqT[:, s, c, dc * P:(dc + 1) * P],
                                 lambda s, c: kpT[:, s, c, h * HB:(h + 1) * HB, :], job_done)
                pe.wait_ge(w_split, 3)
                ctx_keys = ctxT_w.rearrange("p (s c k) -> p s c k", s=2, c=C)
                for step in V_STEPS:
                    if "vt" in step:
                        k, j = step["vt"]
                        ps = bank_free(j)
                        n = KROWS[k]
                        pe.wait_ge(job_drained, base + V_JOB[k] + 1)
                        for c in range(C):
                            last = pe.transpose(ps[:, c * P:c * P + n], v_f[0:n, c * P:(c + 1) * P], ident[0:n, 0:n])
                        last.then_inc(job_done, 1)
                    if "v" in step:
                        k, j = step["v"]
                        ps = bank_free(j)
                        n = KROWS[k]
                        products(ps[0:n, :], lambda s, c: ctx_keys[:, s, c, k * P:k * P + n], lambda s, c: wv_s[:, s, c, :], job_done)
                    if "vg" in step:
                        k, j = step["vg"]
                        ps = bank_free(j)
                        n = KROWS[k]
                        pe.wait_ge(job_drained, base + VT_JOB[k] + 1)
                        products(ps[0:n, :], lambda s, c: vT[:, s, c, 0:n], lambda s, c: wg2_s[:, s, c, :], job_done)

            def turn_x(i, t):
                for c in range(C):
                    last = pe.transpose(turn_ps[t % 2][:, c * P:(c + 1) * P], x_rows[i][:, t, c * P:(c + 1) * P], ident[:, :])
                last.then_inc(x_turned, 1)

            def scores(b, i):
                pe.wait_ge(xT_made, b * T + T)
                pe.wait_ge(mt_split, b + 1)
                for t in range(T):
                    ps = score_ps[:, t * SP:(t + 1) * SP]
                    q = slice(t * P, (t + 1) * P)
                    pe.matmul(ps, row0[:, :], mt_b[i][:, HI, C, :], start=True, stop=False)
                    pe.matmul(ps, row0[:, :], mt_b[i][:, LO, C, :], start=False, stop=False)
                    for c in range(C):
                        for s, m in PRODUCTS:
                            last = pe.matmul(ps, xT[i][:, s, c, q], mt_b[i][:, m, c, :], start=False,
                                             stop=(c == C - 1 and (s, m) == PRODUCTS[-1]))
                last.then_inc(scores_done, 1)

            def gate_main(i, t, chunks):
                q = slice(t * P, (t + 1) * P)
                for c in chunks:
                    for s, m in PRODUCTS:
                        pe.matmul(gate_ps[t % 2][:, :], xT[i][:, s, c, q], wqg[:, m, c, :],
                                  start=(c == 0 and (s, m) == PRODUCTS[0]), stop=False)

            def turn_probs(b):
                pe.wait_ge(prob_split, b + 1)
                pe.wait_ge(prob_stacked_a, b + 1)
                pe.wait_ge(prob_stacked_b, b + 1)
                for t in range(T):
                    last = pe.transpose(turn_a_ps[0:K_A, t * P:(t + 1) * P], w_a[:, t, :], ident[:, :])
                last.then_inc(wa_turned, 1)
                for t in range(T):
                    last = pe.transpose(turn_b_ps[0:K_B, t * P:(t + 1) * P], w_b[:, t, :], ident[:, :])
                last.then_inc(wb_turned, 1)

            def attend(b, i, t):
                q = slice(t * P, (t + 1) * P)
                for ps, cols, done in ((gate_ps[t % 2], slice(D, 2 * D), gate_done), (attn_ps[t % 2], slice(0, D), attn_done)):
                    first = done is attn_done
                    pe.matmul(ps[:, :], wT[0:K_A, 0, q], v_ext[i][0:K_A, 0, cols], start=first, stop=False)
                    pe.matmul(ps[:, :], wT[0:K_B, 1, q], v_ext[i][0:K_B, 1, cols], start=False, stop=True).then_inc(done, 1)

            def batch(b, half, i, more):
                n = 1 - i
                gate_main(i, 0, range(C))
                past(pe, tanh_made, b * T)
                gate_main(i, 1, range(C // 2))
                turn_probs(b)
                gate_main(i, 1, range(C // 2, C))
                pe.wait_ge(wTa_made, b + 1)
                pe.wait_ge(wTb_made, b + 1)
                pe.wait_ge(vext_in[i], half * 64 + 64)
                attend(b, i, 0)

                def turn_next(t):
                    if more:
                        pe.wait_ge(x_in[n][t], (half + i) * 16 + 16)
                        pe.wait_ge(xT_made, b * T + (T + t - 1))
                        turn_x(n, t)

                turn_next(0)
                turn_next(1)
                past(pe, prod_made, b * T)
                attend(b, i, 1)
                pe.wait_ge(tanh_made, b * T + 1)
                gate_main(i, 2, range(C))
                turn_next(2)
                turn_next(3)
                pe.wait_ge(prod_made, b * T + 1)
                attend(b, i, 2)
                if more:
                    scores(b + 1, n)
                pe.wait_ge(tanh_made, b * T + 2)
                gate_main(i, 3, range(C))
                pe.wait_ge(prod_made, b * T + 2)
                attend(b, i, 3)
                if more:
                    pe.wait_ge(tanh_made, b * T + 3)
                    pe.wait_ge(prod_made, b * T + 3)

            for t in range(T):
                pe.wait_ge(x_in[0][t], 16)
                if t >= 2:
                    pe.wait_ge(xT_made, t - 1)
                turn_x(0, t)
            pe.wait_ge(row0_made, 1)
            scores(0, 0)
            pe.wait_ge(job_drained, J_ALL)
            for i in range(2):
                batch(i, 0, i, True)
            with pe.Fori(1, B // 2 - 1) as j:
                for i in range(2):
                    batch(2 * j + i, j, i, True)
            for i in range(2):
                batch(B - 2 + i, B // 2 - 1, i, i == 0)

        @block.scalar
        def _(act):
            def hi_of(ps, dst, job):
                act.wait_ge(job_done, job)
                act.activation(dst, ps, ACT.Copy).then_inc(hi_made, 1)

            for ec in range(C):
                j = J_WQT + ec
                hi_of(bank[j % NBANK][:, :], wqT[:, HI, ec, :], j + 1)
            act.wait_ge(wg1_in, 16)
            act.activation(wg1_s[:, HI], stage[1], ACT.Copy).then_inc(wg1_hi, 1)
            for dc in range(C):
                j = J_WQG + dc
                hi_of(bank[j % NBANK][:, :], wqg[:, HI, dc, :], j + 1)
            act.wait_ge(pads_made, 1)
            act.wait_ge(vec_made, 1)
            with act.Fori(0, G) as g:
                base = g * J_GROUP + J_FIRST
                for c in range(C):
                    for h in range(2):
                        j = J_CTXT + 2 * c + h
                        ps = bank[j % NBANK][:, 0:HK].rearrange("p (b k) -> p b k", b=HB)
                        hi_of(ps[:, :, 0:S], ctxT[:, HI, c, h * HB:(h + 1) * HB, 0:S], base + (j + 1))
                for ec in range(C):
                    for h in range(2):
                        j = J_KPT + 2 * ec + h
                        act.wait_ge(job_done, base + (j + 1))
                        act.activation(kpT[:, HI, ec, h * HB:(h + 1) * HB, :].rearrange("p b k -> p (b k)"), bank[j % NBANK][:, 0:HK],
                                       ACT.Identity, bias=bk_c[:, ec:ec + 1]).then_inc(hi_made, 1)
                for step in V_STEPS:
                    if "vt" in step:
                        k, j = step["vt"]
                        n = KROWS[k]
                        ps = bank[j % NBANK][:, :].rearrange("p (c k) -> p c k", c=C)
                        hi_of(ps[:, :, 0:n], vT[:, HI, :, 0:n], base + (j + 1))
                    for what, src, done, staged, cols in (("v", v_f, v_hi, v_stored, 0), ("vg", vg_f, vg_hi, vg_stored, D)):
                        if what in step:
                            k, j = step[what]
                            n = KROWS[k]
                            act.wait_ge(job_drained, base + (j + 1))
                            if k:
                                act.wait_ge(staged, g * (16 * KT) + 16 * k)
                            act.activation(v_st[0:n, HI, cols:cols + D], src[0:n, :], ACT.Copy).then_inc(done, 1)
                act.wait_ge(v_stored, g * (16 * KT) + 16 * KT)
                act.wait_ge(vg_stored, g * (16 * KT) + 16 * KT)

            def xT_hi_tile(b, i, t):
                act.wait_ge(x_turned, b * T + (t + 1))
                act.activation(xT[i][:, HI, :, t * P:(t + 1) * P], turn_ps[t % 2][:, :].rearrange("p (c q) -> p c q", c=C),
                               ACT.Copy).then_inc(xT_hi, 1)

            def stack_probs(b):
                act.wait_ge(prob_hi, b + 1)
                act.activation(w_a[:, :, S:K_A], w_a[:, :, 0:LO_A], ACT.Copy).then_inc(prob_stacked_a, 1)
                act.activation(w_b[:, :, S:K_B], w_a[:, :, LO_A:S], ACT.Copy).then_inc(prob_stacked_b, 1)

            def exps(b):
                act.wait_ge(shift_made, b + 1)
                act.activation(expd, shifted, ACT.Exp, scale=SCALE).then_inc(exp_made, 1)

            def tanh_tile(b, t):
                act.wait_ge(gate_done, b * T + (t + 1))
                act.activation(tanh_sb[:, t % 2, :], gate_ps[t % 2][:, :], ACT.Tanh, scale=0.5).then_inc(tanh_made, 1)

            def batch(b, i, more):
                act.wait_ge(wa_turned, b + 1)
                act.activation(wT[0:K_A, 0, :], turn_a_ps[0:K_A, :], ACT.Copy).then_inc(wTa_made, 1)
                tanh_tile(b, 0)
                if more:
                    xT_hi_tile(b + 1, 1 - i, 0)
                    xT_hi_tile(b + 1, 1 - i, 1)
                past(act, prod_made, b * T)
                tanh_tile(b, 1)
                if more:
                    xT_hi_tile(b + 1, 1 - i, 2)
                    xT_hi_tile(b + 1, 1 - i, 3)
                act.wait_ge(prod_made, b * T + 1)
                tanh_tile(b, 2)
                if more:
                    exps(b + 1)
                    stack_probs(b + 1)
                act.wait_ge(prod_made, b * T + 2)
                tanh_tile(b, 3)
                if more:
                    act.wait_ge(prod_made, b * T + 3)

            for t in range(T):
                xT_hi_tile(0, 0, t)
            exps(0)
            stack_probs(0)
            for i in range(2):
                batch(i, i, True)
            with act.Fori(1, B // 2 - 1) as j:
                for i in range(2):
                    batch(2 * j + i, i, True)
            for i in range(2):
                batch(B - 2 + i, i, i == 0)

        @block.vector
        def _(dve):
            dve.memset(ones[:, :], 1.0).then_inc(ones_made, 1)
            dve.memset(f32(ctxT[:, :, :, :, S:SP].rearrange("p s c b k -> p (s c b) k")), 0.0).then_inc(pads_made, 1)

            def lo_of(ps, dst_hi, dst_lo, n):
                dve.wait_ge(hi_made, n)
                dve.tensor_tensor(dst_lo, ps, f32(dst_hi), ALU.subtract).then_inc(job_drained, 1)

            dve.wait_ge(job_done, J_VEC + 1)
            dve.tensor_copy(vec[:, :], bank[J_VEC][:, 0:B * T + 2 * C]).then_inc(vec_made, 1)
            dve.wait_ge(vec_made, 1)
            dve.tensor_scalar(half_mask[:, :], vec[:, 0:B * T], 0.5, None, ALU.mult).then_inc(job_drained, 1)
            dve.wait_ge(ones_made, 1)
            for c in range(C):
                last = dve.tensor_scalar(bq_bc[:, HI, c, :], ones[:, :], bq_c[:, c:c + 1], None, ALU.mult)
            last.then_inc(vec_made, 1)
            dve.wait_ge(vec_made, 2)
            for c in range(C):
                last = dve.scalar_tensor_tensor(bq_bc[:, LO, c, :], ones[:, :], bq_c[:, c:c + 1], f32(bq_bc[:, HI, c, :]),
                                                ALU.mult, ALU.subtract)
            last.then_inc(bq_made, 1)
            for ec in range(C):
                lo_of(bank[(J_WQT + ec) % NBANK][:, :], wqT[:, HI, ec, :], wqT[:, LO, ec, :], ec + 1)
            dve.wait_ge(wg1_hi, 1)
            dve.tensor_tensor(wg1_s[:, LO], stage[1], f32(wg1_s[:, HI]), ALU.subtract).then_inc(wg1_split, 1)
            dve.wait_ge(bias_in, 32)
            dve.wait_ge(job_done, J_BTOT + 1)
            dve.tensor_tensor(btot, bank[J_BTOT % NBANK][:, :], btot, ALU.add).then_inc(job_drained, 1)
            for dc in range(C):
                lo_of(bank[(J_WQG + dc) % NBANK][:, :], wqg[:, HI, dc, :], wqg[:, LO, dc, :], C + dc + 1)
            with dve.Fori(0, G) as g:
                base = g * J_GROUP + J_FIRST
                hbase = g * H_GROUP + H_FIRST
                for c in range(C):
                    for h in range(2):
                        j = J_CTXT + 2 * c + h
                        ps = bank[j % NBANK][:, 0:HK].rearrange("p (b k) -> p b k", b=HB)
                        bs = slice(h * HB, (h + 1) * HB)
                        lo_of(ps[:, :, 0:S], ctxT[:, HI, c, bs, 0:S], ctxT[:, LO, c, bs, 0:S], hbase + (H_CTXT + 2 * c + h + 1))
                for ec in range(C):
                    for h in range(2):
                        j = J_KPT + 2 * ec + h
                        hi, lo = (kpT[:, s, ec, h * HB:(h + 1) * HB, :].rearrange("p b k -> p (b k)") for s in (HI, LO))
                        dve.wait_ge(hi_made, hbase + (H_KPT + 2 * ec + h + 1))
                        dve.scalar_tensor_tensor(lo, bank[j % NBANK][:, 0:HK], bk_c[:, ec:ec + 1], f32(hi),
                                                 ALU.add, ALU.subtract).then_inc(job_drained, 1)
                for c in (C, *range(C)):
                    for h in range(2):
                        j = J_SB + h if c == C else J_MT + 2 * c + h
                        dve.wait_ge(job_done, base + (j + 1))
                        dve.tensor_copy(mt[:, bass.ds(g * GB + h * HB, HB), c, :],
                                        bank[j % NBANK][:, 0:HK].rearrange("p (b k) -> p b k", b=HB)).then_inc(job_drained, 1)
                for step in V_STEPS:
                    if "vt" in step:
                        k, j = step["vt"]
                        n = KROWS[k]
                        ps = bank[j % NBANK][:, :].rearrange("p (c k) -> p c k", c=C)
                        lo_of(ps[:, :, 0:n], vT[:, HI, :, 0:n], vT[:, LO, :, 0:n], hbase + (H_VT + k + 1))
                    for what, dst, bias, read in (("v", v_f, bv_bc, v_lo), ("vg", vg_f, btot, vg_lo)):
                        if what in step:
                            k, j = step[what]
                            n = KROWS[k]
                            dve.wait_ge(job_done, base + (j + 1))
                            if k:
                                dve.wait_ge(read, g * KT + k)
                            dve.tensor_tensor(dst[0:n, :], bank[j % NBANK][0:n, :], bias[0:n, :], ALU.add).then_inc(job_drained, 1)
                dve.wait_ge(v_lo, g * KT + KT)
                dve.wait_ge(vg_lo, g * KT + KT)

            def mt_lo(b, i):
                dve.wait_ge(mt_split_hi, b + 1)
                dve.tensor_tensor(mt_b[i][:, LO], mt[:, b], f32(mt_b[i][:, HI]), ALU.subtract).then_inc(mt_split, 1)

            def xT_lo_tile(b, i, t):
                dve.wait_ge(xT_hi, b * T + (t + 1))
                q = slice(t * P, (t + 1) * P)
                dve.tensor_tensor(xT[i][:, LO, :, q], turn_ps[t % 2][:, :].rearrange("p (c q) -> p c q", c=C),
                                  f32(xT[i][:, HI, :, q]), ALU.subtract).then_inc(xT_made, 1)

            def softmax(b):
                sc = score_ps[:, 0:T * SP].rearrange("p (t k) -> p t k", t=T)[:, :, 0:S]
                dve.wait_ge(scores_done, b + 1)
                dve.tensor_reduce(rowmax, sc, AX.X, ALU.max).then_inc(max_made, 1)
                dve.wait_ge(max_made, b + 1)
                dve.tensor_tensor(shifted, sc, rowmax.unsqueeze(2).broadcast_to([P, T, S]), ALU.subtract).then_inc(shift_made, 1)
                dve.wait_ge(exp_made, b + 1)
                dve.tensor_reduce(rowsum, expd, AX.X, ALU.add).then_inc(sum_made, 1)
                dve.wait_ge(sum_made, b + 1)
                dve.reciprocal(rinv, rowsum).then_inc(rinv_made, 1)
                dve.wait_ge(rinv_made, b + 1)
                dve.tensor_tensor(prob, expd, rinv.unsqueeze(2).broadcast_to([P, T, S]), ALU.mult).then_inc(prob_made, 1)
                dve.wait_ge(prob_made, b + 1)
                dve.tensor_copy(w_a[:, :, 0:S].bitcast(F32R), prob).then_inc(prob_hi, 1)
                dve.wait_ge(prob_hi, b + 1)
                dve.tensor_tensor(w_b[:, :, 0:S].bitcast(F32R), prob, w_a[:, :, 0:S], ALU.subtract).then_inc(prob_split, 1)

            def finish(b, t):
                dve.wait_ge(tanh_made, b * T + (t + 1))
                dve.wait_ge(attn_done, b * T + (t + 1))
                dve.scalar_tensor_tensor(prod_sb[:, t % 2, :], tanh_sb[:, t % 2, :], 1.0, attn_ps[t % 2][:, :],
                                         ALU.add, ALU.mult).then_inc(prod_made, 1)
                dve.wait_ge(prod_made, b * T + (t + 1))
                past(dve, stored[t], b * 16)
                hm = half_mask[:, bass.ds(b * T + t, 1)]
                dve.scalar_tensor_tensor(out_sb[:, t, :], prod_sb[:, t % 2, :], hm, x_rows_of[0][:, t, :],
                                         ALU.mult, ALU.add).then_inc(out_made, 1)

            x_rows_of = [None]

            def batch(b, i, more, more2):
                x_rows_of[0] = x_rows[i]
                dve.wait_ge(wb_turned, b + 1)
                dve.tensor_copy(wT[0:K_B, 1, :], turn_b_ps[0:K_B, :]).then_inc(wTb_made, 1)
                finish(b, 0)
                if more:
                    xT_lo_tile(b + 1, 1 - i, 0)
                    xT_lo_tile(b + 1, 1 - i, 1)
                finish(b, 1)
                if more:
                    xT_lo_tile(b + 1, 1 - i, 2)
                    xT_lo_tile(b + 1, 1 - i, 3)
                if more2:
                    mt_lo(b + 2, i)
                finish(b, 2)
                if more:
                    softmax(b + 1)
                finish(b, 3)

            for t in range(T):
                xT_lo_tile(0, 0, t)
            mt_lo(0, 0)
            mt_lo(1, 1)
            softmax(0)
            for i in range(2):
                batch(i, i, True, True)
            with dve.Fori(1, B // 2 - 1) as j:
                for i in range(2):
                    batch(2 * j + i, i, True, True)
            for i in range(2):
                batch(B - 2 + i, i, i == 0, False)

        @block.gpsimd
        def _(pool):
            pool.memset(ident[:, :], 0.0).then_inc(ident_zeroed, 1)
            pool.wait_ge(ident_zeroed, 1)
            pool.affine_select(out=ident[:, :], in_=ident[:, :], compare_op=ALU.not_equal, fill=1.0, base=0,
                               pattern=[[-1, P]], channel_multiplier=1).then_inc(ident_made, 1)
            pool.wait_ge(ones_made, 1)
            pool.affine_select(out=row0[:, :], in_=ones[:, :], compare_op=ALU.is_equal, fill=0.0, base=0,
                               pattern=[[0, P]], channel_multiplier=1).then_inc(row0_made, 1)
            for n, (w, raw, landed) in enumerate(((wk_s, stage[0], wk_in), (wv_s, stage[1], wv_in), (wg2_s, stage[0], wg2_in))):
                pool.wait_ge(landed, 16)
                pool.tensor_copy(w[:, HI], raw).then_inc(w_hi, 1)
                pool.wait_ge(w_hi, n + 1)
                pool.tensor_tensor(w[:, LO], raw, f32(w[:, HI]), ALU.subtract).then_inc(w_split, 1)
            with pool.Fori(0, G) as g:
                for step in V_STEPS:
                    for what, src, hi, lo, cols in (("v", v_f, v_hi, v_lo, 0), ("vg", vg_f, vg_hi, vg_lo, D)):
                        if what in step:
                            k, _ = step[what]
                            n = KROWS[k]
                            pool.wait_ge(hi, g * KT + (k + 1))
                            pool.tensor_tensor(v_st[0:n, LO, cols:cols + D], src[0:n, :], f32(v_st[0:n, HI, cols:cols + D]),
                                               ALU.subtract).then_inc(lo, 1)

            def mt_hi(b, i):
                pool.tensor_copy(mt_b[i][:, HI], mt[:, b]).then_inc(mt_split_hi, 1)

            pool.wait_ge(job_drained, J_ALL)
            mt_hi(0, 0)
            mt_hi(1, 1)

            with pool.Fori(0, B // 2 - 1) as j:
                for i in range(2):
                    pool.wait_ge(scores_done, 2 * j + (i + 1))
                    pool.nop()
                    mt_hi(2 * j + (i + 2), i)


_ARGS = ["x", "ctx_1024", "mask_BxS_ff1", "L0_xattn_Wq", "L0_xattn_bq", "L0_xattn_Wk", "L0_xattn_bk",
         "L0_xattn_Wv", "L0_xattn_bv", "L0_xattn_Wg", "L0_xattn_bg"]


def kernel(**inputs):
    import numpy as np
    import concourse.bacc as bacc
    from concourse.bass_utils import run_bass_kernel_spmd

    nc = bacc.Bacc("TRN2", target_bir_lowering=False, num_devices=1)
    arrays, args = {}, []
    for name in _ARGS:
        a = np.ascontiguousarray(inputs[name])
        arrays[f"in_{name}"] = a
        args.append(nc.dram_tensor(f"in_{name}", a.shape, mybir.dt.from_np(a.dtype), kind="ExternalInput").ap())
    out = nc.dram_tensor("out_y", (B, L, D), F32, kind="ExternalOutput").ap()
    build(nc, *args, out)
    r = run_bass_kernel_spmd(nc, [arrays], core_ids=[0])
    return r.results[0]["out_y"]
```

```python
from contextlib import ExitStack

import concourse.bass as bass
import concourse.mybir as mybir
from concourse.alu_op_type import AluOpType as ALU

F32 = mybir.dt.float32
F32R = mybir.dt.float32r
ACT = mybir.ActivationFunctionType
AX = mybir.AxisListType

P = 128
B, L, D = 16, 512, 512
S = 77
SP = S + 1
C = D // P
T = L // P
HI, LO = 0, 1
SCALE = float(D) ** -0.5

GB = 8
G = B // GB
GK = GB * SP
HB = GB // 2
HK = HB * SP
KT = -(-GK // P)
KROWS = [min(P, GK - k * P) for k in range(KT)]

LO_A = 45
LO_B = S - LO_A
K_A, K_B = S + LO_A, S + LO_B

NBANK = 4
J_VEC = 0
J_WQT = J_VEC + 1
J_WKT = J_WQT + C
J_G = J_WKT + C
J_BTOT = J_G + C
J_WQG = J_BTOT + 1
J_FIRST = J_WQG + C
H_FIRST = 4 * C


def group_jobs():
    jobs = [("ctxT", c, 0) for c in range(C)]
    for c in range(C):
        jobs += [("mt", c, 0), ("ctxT", c, 1)]
    jobs += [("sb", 0, 0)] + [("mt", c, 1) for c in range(C)] + [("sb", 0, 1)]
    for k in range(KT + 1):
        if k >= 1:
            jobs.append(("vT", k - 1, 0))
        if k < KT:
            jobs.append(("v", k, 0))
        if k >= 1:
            jobs.append(("vg", k - 1, 0))
    return jobs


JOBS = group_jobs()
J_GROUP = len(JOBS)
SPLIT_KINDS = ("ctxT", "vT")
H_GROUP = sum(j[0] in SPLIT_KINDS for j in JOBS)
HI_NUMBER = {j: sum(i[0] in SPLIT_KINDS for i in JOBS[:n]) for n, j in enumerate(JOBS)}
NUMBER = {j: n for n, j in enumerate(JOBS)}
J_ALL = J_FIRST + G * J_GROUP

PRODUCTS = [(HI, HI), (HI, LO), (LO, HI)]


def build(nc, x, ctx_in, mask, wq, bq, wk, bk, wv, bv, wg, bg, out):
    with ExitStack() as es:
        def sb(name, shape, dt=F32):
            return es.enter_context(nc.sbuf_tensor(name, shape, dt))

        def sem(name):
            return es.enter_context(nc.semaphore(name))

        bank = [es.enter_context(nc.psum_tensor(f"bank{i}", [P, 512], F32)) for i in range(8)]
        gate_ps, attn_ps, turn_ps = bank[0:2], bank[2:4], bank[4:6]
        score_ps, turn_a_ps = bank[6], bank[7]
        turn_b_ps = score_ps
        sT_ps = turn_a_ps

        v_dram = nc.dram_tensor("v_scratch", [B * SP, 2, 2 * D], F32, kind="Internal").ap()

        W_HL = 2 * C * D
        XT_WORDS = 2 * C * L
        SLOTS = 5
        arena_r = sb("arena_r", [P, 2 * C * GK + SLOTS * W_HL + 2 * D + 2 * 2 * D], F32R)
        at = [0]

        def take(words):
            at[0] += words
            return arena_r[:, at[0] - words:at[0]]

        def split_w(words):
            return words.rearrange("p (s c n) -> p s c n", s=2, c=C)

        ctxT_w = take(2 * C * GK)
        slot = [take(W_HL) for _ in range(SLOTS)]
        vT = take(2 * D).rearrange("p (s c k) -> p s c k", s=2, c=C)
        v_st = take(2 * 2 * D).rearrange("p (s n) -> p s n", s=2)
        ctxT = ctxT_w.rearrange("p (s c b k) -> p s c b k", s=2, c=C, b=GB)
        wkT, wqT, g_s, wg1_s, wg2_s = (split_w(w) for w in slot)
        wv_s = wkT
        wqg = sb("wqg", [P, 2, C, D], F32R)
        bq_bc = sb("bq_bc", [P, 2, C, P], F32R)
        u_bc = sb("u_bc", [P, 2, C, P], F32R)
        xT = [slot[i][:, 0:XT_WORDS].rearrange("p (s c q) -> p s c q", s=2, c=C) for i in (0, 1)]
        v_ext = [ctxT_w[:, i * 4 * D:(i + 1) * 4 * D].rearrange("p (h n) -> p h n", h=2) for i in range(2)]
        wT = slot[3][:, 0:2 * L].rearrange("p (h q) -> p h q", h=2)
        mt_b = [sb(f"mt_b{i}", [P, 2, C, SP], F32R) for i in range(2)]

        rows_w = sb("rows_w", [P, 2, C * D])
        stage = [rows_w[:, i, :].rearrange("p (c n) -> p c n", c=C) for i in range(2)]
        x_rows = [rows_w[:, i, :].rearrange("p (t n) -> p t n", t=T) for i in range(2)]
        work = sb("work", [P, GB * D])
        ctx_rows = work[:, :].rearrange("p (b n) -> p b n", b=GB)
        out_sb = work[:, 0:T * D].rearrange("p (t n) -> p t n", t=T)
        tanh_sb = work[:, T * D:(T + 2) * D].rearrange("p (i n) -> p i n", i=2)
        prod_sb = work[:, (T + 2) * D:(T + 4) * D].rearrange("p (i n) -> p i n", i=2)
        mt = sb("mt", [P, B, C, SP])
        sb_c = sb("sb_c", [SP, B])
        sb_diag = sb("sb_diag", [SP, HB, SP])
        sT_raw = sb("sT", [P, L])
        sT = sT_raw[0:S, :]
        small = sb("small", [P, 4 * D])
        v_f, vg_f, bv_bc, btot = (small[:, i * D:(i + 1) * D] for i in range(4))
        o = 0
        soft = []
        for n in (T * S, T * S, T * S, T * K_A, T * K_B):
            soft.append(small[:, o:o + n].rearrange("p (t k) -> p t k", t=T))
            o += n
        shifted, expd, prob, w_a, w_b = soft
        dot_tmp = sT_raw[:, :]
        sb_sum = sb("sb_sum", [SP, HB])
        stat = sb("stat", [P, 3, T])
        rowmax, rowsum, rinv = stat[:, 0, :], stat[:, 1, :], stat[:, 2, :]
        bq_row, bk_row = v_f, vg_f
        u_c, wqbk_c, bqbk = sb("u_c", [P, C]), sb("wqbk_c", [P, C]), sb("bqbk", [P, 1])
        ident = sb("ident", [P, P])
        ones = sb("ones", [P, P])
        vec_rows = sb("vec_rows", [B * T + C, P])
        vec = sb("vec", [P, B * T + C])
        bq_c = vec[:, B * T:B * T + C]
        half_mask = sb("half_mask", [P, B * T])

        wq_in, wg1_in, wk_in, wv_in, wg2_in = (sem(n) for n in ("wq_in", "wg1_in", "wk_in", "wv_in", "wg2_in"))
        vec_in, brow_in, bias_in, ctx_in_s = sem("vec_in"), sem("brow_in"), sem("bias_in"), sem("ctx_in_s")
        dots_made, u_hi, u_made, diag_made, sb_made = (sem(n) for n in ("dots_made", "u_hi", "u_made", "diag_made", "sb_made"))
        ones_made, ident_zeroed, ident_made = sem("ones_made"), sem("ident_zeroed"), sem("ident_made")
        vec_made, bq_hi, bq_made, pads_made = sem("vec_made"), sem("bq_hi"), sem("bq_made"), sem("pads_made")
        job_done = sem("job_done")
        hi_made = sem("hi_made")
        job_drained = sem("job_drained")
        w_hi, w_split = sem("w_hi"), sem("w_split")
        v_hi, v_lo, vg_hi, vg_lo = sem("v_hi"), sem("v_lo"), sem("vg_hi"), sem("vg_lo")
        v_stored, vg_stored = sem("v_stored"), sem("vg_stored")
        x_in = [[sem(f"x_in{i}{t}") for t in range(T)] for i in range(2)]
        vext_in = [sem(f"vext_in{i}") for i in range(2)]
        mt_split_hi, mt_split = sem("mt_split_hi"), sem("mt_split")
        x_turned, xT_hi, xT_made = sem("x_turned"), sem("xT_hi"), sem("xT_made")
        sT_done, sT_made, scores_done = sem("sT_done"), sem("sT_made"), sem("scores_done")
        max_made, shift_made, exp_made = sem("max_made"), sem("shift_made"), sem("exp_made")
        sum_made, rinv_made, prob_made = sem("sum_made"), sem("rinv_made"), sem("prob_made")
        prob_hi, prob_split = sem("prob_hi"), sem("prob_split")
        prob_stacked_a, prob_stacked_b = sem("prob_stacked_a"), sem("prob_stacked_b")
        wa_turned, wb_turned, wTa_made, wTb_made = sem("wa_turned"), sem("wb_turned"), sem("wTa_made"), sem("wTb_made")
        gate_done, attn_done = sem("gate_done"), sem("attn_done")
        tanh_made, prod_made, out_made = sem("tanh_made"), sem("prod_made"), sem("out_made")
        stored = [sem(f"stored{t}") for t in range(T)]

        x_v = x.rearrange("b (t p) d -> b t p d", p=P)
        out_v = out.rearrange("b (t p) d -> b t p d", p=P)

        def w_rows(w):
            return w.rearrange("(c p) n -> p c n", p=P)

        def f32(ap):
            return ap.bitcast(F32)

        def past(eng, sem_, value):
            if not isinstance(value, int) or value > 0:
                eng.wait_ge(sem_, value)

        block = es.enter_context(nc.Block())

        @block.sync
        def _(sync):
            sync.dma_start(stage[0], w_rows(wq)).then_inc(wq_in, 16)
            sync.dma_start(vec_rows[0:B * T, :], mask.rearrange("b (t p) -> (b t) p", p=P)).then_inc(vec_in, 16)
            sync.dma_start(vec_rows[B * T:B * T + C, :], bq.rearrange("(c p) -> c p", p=P)).then_inc(vec_in, 16)
            sync.dma_start(stage[1], w_rows(wk)).then_inc(wk_in, 16)
            for row, b_ in ((bq_row, bq), (bk_row, bk)):
                sync.dma_start(row, b_.rearrange("(a n) -> a n", a=1).broadcast_to([P, D])).then_inc(brow_in, 16)
            for row, b_ in ((btot, bg), (bv_bc, bv)):
                sync.dma_start(row, b_.rearrange("(a n) -> a n", a=1).broadcast_to([P, D])).then_inc(bias_in, 16)
            sync.wait_ge(job_done, J_WQT + C)
            sync.wait_ge(dots_made, C)
            sync.dma_start(stage[0], w_rows(wg[0:D, :])).then_inc(wg1_in, 16)
            sync.dma_start(ctx_rows[0:S], ctx_in[0:GB].rearrange("b k d -> k b d")).then_inc(ctx_in_s, 16)
            sync.wait_ge(job_done, J_WKT + C)
            sync.wait_ge(dots_made, 2 * C)
            sync.dma_start(stage[1], w_rows(wv)).then_inc(wv_in, 16)
            sync.wait_ge(w_split, 1)
            sync.dma_start(stage[0], w_rows(wg[D:2 * D, :])).then_inc(wg2_in, 16)
            sync.wait_ge(w_split, 3)
            for b in range(2):
                for t in range(T):
                    sync.dma_start(x_rows[b][:, t, :], x_v[b, t]).then_inc(x_in[b][t], 16)
            for g in range(G):
                if g + 1 < G:
                    sync.wait_ge(job_done, J_FIRST + g * J_GROUP + NUMBER["ctxT", C - 1, 1] + 1)
                    sync.dma_start(ctx_rows[0:S], ctx_in[(g + 1) * GB:(g + 2) * GB].rearrange("b k d -> k b d")).then_inc(ctx_in_s, 16)
                for kind, k, _ in JOBS:
                    if kind in ("v", "vg"):
                        made, done, cols = (v_lo, v_stored, 0) if kind == "v" else (vg_lo, vg_stored, D)
                        r0 = g * GK + k * P
                        sync.wait_ge(made, g * KT + k + 1)
                        sync.dma_start(v_dram[r0:r0 + KROWS[k], :, cols:cols + D],
                                       f32(v_st[0:KROWS[k], :, cols:cols + D])).then_inc(done, 16)

            def load_vext(b, i):
                r = b * SP
                for h, lo0, n in ((0, 0, LO_A), (1, LO_A, LO_B)):
                    sync.dma_start(f32(v_ext[i][0:S, h, :]), v_dram[bass.ds(r, S), HI, :]).then_inc(vext_in[i], 16)
                    sync.dma_start(f32(v_ext[i][S:S + n, h, :]), v_dram[bass.ds(r + lo0, n), LO, :]).then_inc(vext_in[i], 16)

            sync.wait_ge(v_stored, 16 * G * KT)
            sync.wait_ge(vg_stored, 16 * G * KT)
            sync.wait_ge(job_done, J_ALL)
            for b in range(2):
                load_vext(b, b)

            def batch(b, i, more):
                for t in range(T):
                    sync.wait_ge(out_made, b * T + (t + 1))
                    sync.dma_start(out_v[b, t], out_sb[:, t, :]).then_inc(stored[t], 16)
                    if more:
                        sync.dma_start(x_rows[i][:, t, :], x_v[b + 2, t]).then_inc(x_in[i][t], 16)
                if more:
                    sync.wait_ge(attn_done, b * T + T)
                    load_vext(b + 2, i)

            for i in range(2):
                batch(i, i, True)
            with sync.Fori(1, B // 2 - 1) as j:
                for i in range(2):
                    batch(2 * j + i, i, True)
            for i in range(2):
                batch(B - 2 + i, i, False)
            for t in range(T):
                sync.wait_ge(stored[t], 16 * B)

        @block.tensor
        def _(pe):
            def products(ps, lhs, rhs, sem_, inc=1):
                n, last = 0, None
                for c in range(C):
                    for s, m in PRODUCTS:
                        last = pe.matmul(ps, lhs(s, c), rhs(m, c), start=(n == 0), stop=(n == 3 * C - 1))
                        n += 1
                if sem_ is not None:
                    last.then_inc(sem_, inc)

            pe.wait_ge(ident_made, 1)
            pe.wait_ge(vec_in, 32)
            NV = B * T + C
            pe.transpose(bank[J_VEC][:, 0:NV], vec_rows[:, :], ident[0:NV, 0:NV]).then_inc(job_done, 1)
            for landed, raw, first in ((wq_in, stage[0], J_WQT), (wk_in, stage[1], J_WKT)):
                pe.wait_ge(landed, 16)
                for ec in range(C):
                    j = first + ec
                    if j >= NBANK:
                        pe.wait_ge(job_drained, j - NBANK + 1)
                    for rc in range(C):
                        last = pe.transpose(bank[j % NBANK][:, rc * P:(rc + 1) * P], raw[:, rc, ec * P:(ec + 1) * P], ident[:, :])
                    last.then_inc(job_done, 1)
            for cc in range(C):
                j = J_G + cc
                pe.wait_ge(job_drained, J_WKT + C)
                products(bank[j % NBANK][:, :], lambda s, c: wkT[:, s, c, cc * P:(cc + 1) * P],
                         lambda s, c: wqT[:, s, c, :], job_done)
            pe.wait_ge(w_split, 1)
            pe.wait_ge(bq_made, 1)
            pe.wait_ge(job_drained, J_BTOT - NBANK + 1)
            products(bank[J_BTOT % NBANK][:, :], lambda s, c: bq_bc[:, s, c, :], lambda s, c: wg1_s[:, s, c, :], job_done)
            for dc in range(C):
                j = J_WQG + dc
                pe.wait_ge(job_drained, j - NBANK + 1)
                products(bank[j % NBANK][:, :], lambda s, c: wqT[:, s, c, dc * P:(dc + 1) * P],
                         lambda s, c: wg1_s[:, s, c, :], job_done)

            with pe.Fori(0, G) as g:
                base = g * J_GROUP + J_FIRST
                pe.wait_ge(ctx_in_s, g * 16 + 16)
                ctx_keys = ctxT_w.rearrange("p (s c k) -> p s c k", s=2, c=C)
                for j, (kind, k, h) in enumerate(JOBS):
                    free = max(j - NBANK + 1, 0)
                    if kind in ("mt", "sb"):
                        free = max(free, NUMBER["ctxT", C - 1, h] + 1)
                    if kind == "vT":
                        free = max(free, NUMBER["v", k, 0] + 1)
                    if kind == "vg":
                        free = max(free, NUMBER["vT", k, 0] + 1)
                    if kind == "sb" and h == 0:
                        pe.wait_ge(u_made, 1)
                    if kind == "v" and k == 0:
                        pe.wait_ge(w_split, 3)
                    pe.wait_ge(job_drained, base + free)
                    ps = bank[j % NBANK]
                    hs = slice(h * HB, (h + 1) * HB)
                    n = KROWS[k] if kind in ("v", "vT", "vg") else P
                    if kind == "ctxT":
                        for i in range(HB):
                            last = pe.transpose(ps[:, i * SP:i * SP + S], ctx_rows[0:S, h * HB + i, k * P:(k + 1) * P], ident[0:S, 0:S])
                        last.then_inc(job_done, 1)
                    elif kind == "mt":
                        products(ps[:, 0:HK], lambda s, c: g_s[:, s, c, k * P:(k + 1) * P],
                                 lambda s, c: ctxT[:, s, c, hs, :], job_done)
                    elif kind == "sb":
                        products(ps[:, 0:HK], lambda s, c: u_bc[:, s, c, :], lambda s, c: ctxT[:, s, c, hs, :], job_done)
                    elif kind == "vT":
                        for c in range(C):
                            last = pe.transpose(ps[:, c * P:c * P + n], v_f[0:n, c * P:(c + 1) * P], ident[0:n, 0:n])
                        last.then_inc(job_done, 1)
                    elif kind == "v":
                        products(ps[0:n, :], lambda s, c: ctx_keys[:, s, c, k * P:k * P + n], lambda s, c: wv_s[:, s, c, :], job_done)
                    elif kind == "vg":
                        products(ps[0:n, :], lambda s, c: vT[:, s, c, 0:n], lambda s, c: wg2_s[:, s, c, :], job_done)

            def turn_x(i, t):
                for c in range(C):
                    last = pe.transpose(turn_ps[t % 2][:, c * P:(c + 1) * P], x_rows[i][:, t, c * P:(c + 1) * P], ident[:, :])
                last.then_inc(x_turned, 1)

            def scores_T(b, i):
                pe.wait_ge(xT_made, b * T + T)
                pe.wait_ge(mt_split, b + 1)
                products(sT_ps[0:S, :], lambda s, c: mt_b[i][:, s, c, 0:S], lambda s, c: xT[i][:, s, c, :], sT_done)

            def turn_scores(b):
                pe.wait_ge(sT_made, b + 1)
                for t in range(T):
                    last = pe.transpose(score_ps[:, t * S:(t + 1) * S], sT[:, t * P:(t + 1) * P], ident[0:S, 0:S])
                last.then_inc(scores_done, 1)

            def gate_main(i, t, chunks):
                q = slice(t * P, (t + 1) * P)
                for c in chunks:
                    for s, m in PRODUCTS:
                        pe.matmul(gate_ps[t % 2][:, :], xT[i][:, s, c, q], wqg[:, m, c, :],
                                  start=(c == 0 and (s, m) == PRODUCTS[0]), stop=False)

            def turn_probs(b):
                pe.wait_ge(prob_split, b + 1)
                pe.wait_ge(prob_stacked_a, b + 1)
                pe.wait_ge(prob_stacked_b, b + 1)
                for t in range(T):
                    last = pe.transpose(turn_a_ps[0:K_A, t * P:(t + 1) * P], w_a[:, t, :], ident[:, :])
                last.then_inc(wa_turned, 1)
                for t in range(T):
                    last = pe.transpose(turn_b_ps[0:K_B, t * P:(t + 1) * P], w_b[:, t, :], ident[:, :])
                last.then_inc(wb_turned, 1)

            def attend(b, i, t):
                q = slice(t * P, (t + 1) * P)
                for ps, cols, done in ((gate_ps[t % 2], slice(D, 2 * D), gate_done), (attn_ps[t % 2], slice(0, D), attn_done)):
                    first = done is attn_done
                    pe.matmul(ps[:, :], wT[0:K_A, 0, q], v_ext[i][0:K_A, 0, cols], start=first, stop=False)
                    pe.matmul(ps[:, :], wT[0:K_B, 1, q], v_ext[i][0:K_B, 1, cols], start=False, stop=True).then_inc(done, 1)

            def batch(b, half, i, more):
                n = 1 - i
                if not (isinstance(b, int) and b == 0):
                    gate_main(i, 0, range(C))
                    pe.wait_ge(tanh_made, b * T)
                    gate_main(i, 1, range(C // 2))
                turn_probs(b)
                if not (isinstance(b, int) and b == 0):
                    gate_main(i, 1, range(C // 2, C))
                pe.wait_ge(wTa_made, b + 1)
                pe.wait_ge(wTb_made, b + 1)
                pe.wait_ge(vext_in[i], half * 64 + 64)
                attend(b, i, 0)

                def turn_next(t):
                    if more:
                        pe.wait_ge(x_in[n][t], (half + i) * 16 + 16)
                        pe.wait_ge(xT_made, b * T + (T + t - 1))
                        turn_x(n, t)

                turn_next(0)
                turn_next(1)
                past(pe, prod_made, b * T)
                attend(b, i, 1)
                turn_next(2)
                turn_next(3)
                pe.wait_ge(tanh_made, b * T + 1)
                gate_main(i, 2, range(C))
                pe.wait_ge(prod_made, b * T + 1)
                attend(b, i, 2)
                if more:
                    scores_T(b + 1, n)
                pe.wait_ge(tanh_made, b * T + 2)
                gate_main(i, 3, range(C))
                if more:
                    turn_scores(b + 1)
                pe.wait_ge(prod_made, b * T + 2)
                attend(b, i, 3)
                if more:
                    pe.wait_ge(tanh_made, b * T + 3)
                    pe.wait_ge(prod_made, b * T + 3)

            for t in range(T):
                pe.wait_ge(x_in[0][t], 16)
                if t >= 2:
                    pe.wait_ge(xT_made, t - 1)
                turn_x(0, t)
                if t == 2:
                    pe.wait_ge(job_drained, J_ALL)
                    gate_main(0, 0, range(C))
            scores_T(0, 0)
            gate_main(0, 1, range(C))
            turn_scores(0)
            for i in range(2):
                batch(i, 0, i, True)
            with pe.Fori(1, B // 2 - 1) as j:
                for i in range(2):
                    batch(2 * j + i, j, i, True)
            for i in range(2):
                batch(B - 2 + i, B // 2 - 1, i, i == 0)

        @block.scalar
        def _(act):
            def hi_of(ps, dst, job):
                act.wait_ge(job_done, job)
                act.activation(dst, ps, ACT.Copy).then_inc(hi_made, 1)

            def split_hi(dst, raw, landed):
                act.wait_ge(landed, 16)
                act.activation(dst[:, HI], raw, ACT.Copy).then_inc(w_hi, 1)

            for first, dst in ((J_WQT, wqT), (J_WKT, wkT), (J_G, g_s)):
                for c in range(C):
                    j = first + c
                    hi_of(bank[j % NBANK][:, :], dst[:, HI, c, :], j + 1)
                    if j == J_G + 1:
                        split_hi(wg1_s, stage[0], wg1_in)
            for dc in range(C):
                j = J_WQG + dc
                hi_of(bank[j % NBANK][:, :], wqg[:, HI, dc, :], j + 1)
                if dc == 0:
                    split_hi(wv_s, stage[1], wv_in)
                if dc == 2:
                    split_hi(wg2_s, stage[0], wg2_in)
            act.wait_ge(pads_made, 1)
            with act.Fori(0, G) as g:
                base = g * J_GROUP + J_FIRST
                for j, (kind, k, h) in enumerate(JOBS):
                    if kind == "ctxT":
                        ps = bank[j % NBANK][:, 0:HK].rearrange("p (b k) -> p b k", b=HB)
                        hi_of(ps[:, :, 0:S], ctxT[:, HI, k, h * HB:(h + 1) * HB, 0:S], base + (j + 1))
                    elif kind == "vT":
                        n = KROWS[k]
                        ps = bank[j % NBANK][:, :].rearrange("p (c k) -> p c k", c=C)
                        hi_of(ps[:, :, 0:n], vT[:, HI, :, 0:n], base + (j + 1))
                    elif kind in ("v", "vg"):
                        src, done, staged, cols = (v_f, v_hi, v_stored, 0) if kind == "v" else (vg_f, vg_hi, vg_stored, D)
                        n = KROWS[k]
                        act.wait_ge(job_drained, base + (j + 1))
                        if k:
                            act.wait_ge(staged, g * (16 * KT) + 16 * k)
                        act.activation(v_st[0:n, HI, cols:cols + D], src[0:n, :], ACT.Copy).then_inc(done, 1)
                act.wait_ge(v_stored, g * (16 * KT) + 16 * KT)
                act.wait_ge(vg_stored, g * (16 * KT) + 16 * KT)

            def xT_hi_tile(b, i, t):
                act.wait_ge(x_turned, b * T + (t + 1))
                act.activation(xT[i][:, HI, :, t * P:(t + 1) * P], turn_ps[t % 2][:, :].rearrange("p (c q) -> p c q", c=C),
                               ACT.Copy).then_inc(xT_hi, 1)

            def stack_probs(b):
                act.wait_ge(prob_hi, b + 1)
                act.activation(w_a[:, :, S:K_A], w_a[:, :, 0:LO_A], ACT.Copy).then_inc(prob_stacked_a, 1)
                act.activation(w_b[:, :, S:K_B], w_a[:, :, LO_A:S], ACT.Copy).then_inc(prob_stacked_b, 1)

            def exps(b):
                act.wait_ge(shift_made, b + 1)
                act.activation(expd, shifted, ACT.Exp, scale=SCALE).then_inc(exp_made, 1)

            def tanh_tile(b, t):
                act.wait_ge(gate_done, b * T + (t + 1))
                act.activation(tanh_sb[:, t % 2, :], gate_ps[t % 2][:, :], ACT.Tanh, scale=0.5).then_inc(tanh_made, 1)

            def batch(b, i, more):
                act.wait_ge(wa_turned, b + 1)
                act.activation(wT[0:K_A, 0, :], turn_a_ps[0:K_A, :], ACT.Copy).then_inc(wTa_made, 1)
                act.wait_ge(wb_turned, b + 1)
                act.activation(wT[0:K_B, 1, :], turn_b_ps[0:K_B, :], ACT.Copy).then_inc(wTb_made, 1)
                tanh_tile(b, 0)
                if more:
                    xT_hi_tile(b + 1, 1 - i, 0)
                    xT_hi_tile(b + 1, 1 - i, 1)
                past(act, prod_made, b * T)
                tanh_tile(b, 1)
                if more:
                    xT_hi_tile(b + 1, 1 - i, 2)
                    xT_hi_tile(b + 1, 1 - i, 3)
                act.wait_ge(prod_made, b * T + 1)
                tanh_tile(b, 2)
                if more:
                    exps(b + 1)
                    stack_probs(b + 1)
                act.wait_ge(prod_made, b * T + 2)
                tanh_tile(b, 3)
                if more:
                    act.wait_ge(prod_made, b * T + 3)

            for t in range(T):
                xT_hi_tile(0, 0, t)
            exps(0)
            stack_probs(0)
            for i in range(2):
                batch(i, i, True)
            with act.Fori(1, B // 2 - 1) as j:
                for i in range(2):
                    batch(2 * j + i, i, True)
            for i in range(2):
                batch(B - 2 + i, i, i == 0)

        @block.vector
        def _(dve):
            dve.memset(ones[:, :], 1.0).then_inc(ones_made, 1)
            dve.memset(f32(ctxT[:, :, :, :, S:SP].rearrange("p s c b k -> p (s c b) k")), 0.0).then_inc(pads_made, 1)

            def lo_of(ps, dst_hi, dst_lo, n):
                dve.wait_ge(hi_made, n)
                dve.tensor_tensor(dst_lo, ps, f32(dst_hi), ALU.subtract).then_inc(job_drained, 1)

            def split_lo(dst, raw, n):
                dve.wait_ge(w_hi, n)
                dve.tensor_tensor(dst[:, LO], raw, f32(dst[:, HI]), ALU.subtract).then_inc(w_split, 1)

            def dots(raw, row, dst, n):
                for c in range(C):
                    if n + c:
                        dve.wait_ge(dots_made, n + c)
                    dve.tensor_tensor_reduce(dot_tmp, raw[:, c, :], row, 1.0, 0.0, ALU.mult, ALU.add,
                                             dst[:, c:c + 1]).then_inc(dots_made, 1)

            def broadcast(dst, col, hi_sem, made):
                for c in range(C):
                    last = dve.tensor_scalar(dst[:, HI, c, :], ones[:, :], col[:, c:c + 1], None, ALU.mult)
                last.then_inc(hi_sem, 1)
                dve.wait_ge(hi_sem, 1)
                for c in range(C):
                    last = dve.scalar_tensor_tensor(dst[:, LO, c, :], ones[:, :], col[:, c:c + 1], f32(dst[:, HI, c, :]),
                                                    ALU.mult, ALU.subtract)
                last.then_inc(made, 1)

            dve.wait_ge(job_done, J_VEC + 1)
            dve.tensor_copy(vec[:, :], bank[J_VEC][:, 0:B * T + C]).then_inc(vec_made, 1)
            dve.wait_ge(vec_made, 1)
            dve.tensor_scalar(half_mask[:, :], vec[:, 0:B * T], 0.5, None, ALU.mult).then_inc(job_drained, 1)
            for ec in range(C):
                lo_of(bank[(J_WQT + ec) % NBANK][:, :], wqT[:, HI, ec, :], wqT[:, LO, ec, :], ec + 1)
            dve.wait_ge(brow_in, 32)
            dve.wait_ge(wq_in, 16)
            dots(stage[0], bk_row, wqbk_c, 0)
            for ec in range(C):
                lo_of(bank[(J_WKT + ec) % NBANK][:, :], wkT[:, HI, ec, :], wkT[:, LO, ec, :], C + ec + 1)
            dve.wait_ge(wk_in, 16)
            dots(stage[1], bq_row, u_c, C)
            dve.wait_ge(dots_made, 2 * C)
            dve.tensor_tensor_reduce(dot_tmp, bq_row, bk_row, 1.0, 0.0, ALU.mult, ALU.add, bqbk[:, 0:1]).then_inc(dots_made, 1)
            dve.wait_ge(ones_made, 1)
            broadcast(bq_bc, bq_c, bq_hi, bq_made)
            for cc in range(C):
                lo_of(bank[(J_G + cc) % NBANK][:, :], g_s[:, HI, cc, :], g_s[:, LO, cc, :], 2 * C + cc + 1)
                if cc == 1:
                    split_lo(wg1_s, stage[0], 1)
            dve.wait_ge(dots_made, 2 * C)
            broadcast(u_bc, u_c, u_hi, u_made)
            dve.wait_ge(bias_in, 32)
            dve.wait_ge(job_done, J_BTOT + 1)
            dve.tensor_tensor(btot, bank[J_BTOT % NBANK][:, :], btot, ALU.add).then_inc(job_drained, 1)
            for dc in range(C):
                lo_of(bank[(J_WQG + dc) % NBANK][:, :], wqg[:, HI, dc, :], wqg[:, LO, dc, :], 3 * C + dc + 1)
                if dc == 0:
                    split_lo(wv_s, stage[1], 2)
                if dc == 2:
                    split_lo(wg2_s, stage[0], 3)
            dve.wait_ge(dots_made, 2 * C + 1)
            with dve.Fori(0, G) as g:
                base = g * J_GROUP + J_FIRST
                hbase = g * H_GROUP + H_FIRST

                def stage_lo(kind, k):
                    src, hi, lo, cols = (v_f, v_hi, v_lo, 0) if kind == "v" else (vg_f, vg_hi, vg_lo, D)
                    n = KROWS[k]
                    dve.wait_ge(hi, g * KT + (k + 1))
                    dve.tensor_tensor(v_st[0:n, LO, cols:cols + D], src[0:n, :], f32(v_st[0:n, HI, cols:cols + D]),
                                      ALU.subtract).then_inc(lo, 1)

                for j, (kind, k, h) in enumerate(JOBS):
                    ps = bank[j % NBANK]
                    ps_b = ps[:, 0:HK].rearrange("p (b k) -> p b k", b=HB)
                    if kind == "ctxT":
                        bs = slice(h * HB, (h + 1) * HB)
                        lo_of(ps_b[:, :, 0:S], ctxT[:, HI, k, bs, 0:S], ctxT[:, LO, k, bs, 0:S], hbase + (HI_NUMBER[kind, k, h] + 1))
                    elif kind == "vT":
                        n = KROWS[k]
                        ps_c = ps[:, :].rearrange("p (c k) -> p c k", c=C)
                        lo_of(ps_c[:, :, 0:n], vT[:, HI, :, 0:n], vT[:, LO, :, 0:n], hbase + (HI_NUMBER[kind, k, h] + 1))
                    elif kind == "mt":
                        dve.wait_ge(job_done, base + (j + 1))
                        dve.tensor_scalar(mt[:, bass.ds(g * GB + h * HB, HB), k, :], ps_b, wqbk_c[:, k:k + 1], None,
                                          ALU.add).then_inc(job_drained, 1)
                    elif kind == "sb":
                        dve.wait_ge(job_done, base + (j + 1))
                        dve.tensor_tensor(sb_diag[:, :, :], ps_b[0:SP], ident[0:SP, 0:SP].unsqueeze(1).broadcast_to([SP, HB, SP]),
                                          ALU.mult).then_inc(job_drained, 1)
                        dve.wait_ge(job_drained, base + (j + 1))
                        dve.tensor_reduce(sb_sum[:, :], sb_diag[:, :, :], AX.X, ALU.add).then_inc(diag_made, 1)
                        dve.wait_ge(diag_made, g * 2 + (h + 1))
                        dve.tensor_scalar(sb_c[:, bass.ds(g * GB + h * HB, HB)], sb_sum[:, :], bqbk[0:SP, 0:1], None,
                                          ALU.add).then_inc(sb_made, 1)
                    else:
                        n = KROWS[k]
                        dst, bias, read = (v_f, bv_bc, v_lo) if kind == "v" else (vg_f, btot, vg_lo)
                        if k:
                            dve.wait_ge(read, g * KT + k)
                        dve.wait_ge(job_done, base + (j + 1))
                        dve.tensor_tensor(dst[0:n, :], ps[0:n, :], bias[0:n, :], ALU.add).then_inc(job_drained, 1)
                        if kind == "vg":
                            if k + 1 < KT:
                                stage_lo("v", k + 1)
                            stage_lo("vg", k)
                        elif k == 0:
                            stage_lo("v", 0)
                dve.wait_ge(v_lo, g * KT + KT)
                dve.wait_ge(vg_lo, g * KT + KT)

            def mt_lo(b, i):
                dve.wait_ge(mt_split_hi, b + 1)
                dve.tensor_tensor(mt_b[i][:, LO], mt[:, b], f32(mt_b[i][:, HI]), ALU.subtract).then_inc(mt_split, 1)

            def xT_lo_tile(b, i, t):
                dve.wait_ge(xT_hi, b * T + (t + 1))
                q = slice(t * P, (t + 1) * P)
                dve.tensor_tensor(xT[i][:, LO, :, q], turn_ps[t % 2][:, :].rearrange("p (c q) -> p c q", c=C),
                                  f32(xT[i][:, HI, :, q]), ALU.subtract).then_inc(xT_made, 1)

            def add_sb(b):
                dve.wait_ge(sT_done, b + 1)
                dve.tensor_scalar(sT, sT_ps[0:S, :], sb_c[0:S, bass.ds(b, 1)], None, ALU.add).then_inc(sT_made, 1)

            def softmax(b):
                sc = score_ps[:, 0:T * S].rearrange("p (t k) -> p t k", t=T)
                dve.wait_ge(scores_done, b + 1)
                dve.tensor_reduce(rowmax, sc, AX.X, ALU.max).then_inc(max_made, 1)
                dve.wait_ge(max_made, b + 1)
                dve.tensor_tensor(shifted, sc, rowmax.unsqueeze(2).broadcast_to([P, T, S]), ALU.subtract).then_inc(shift_made, 1)
                dve.wait_ge(exp_made, b + 1)
                dve.tensor_reduce(rowsum, expd, AX.X, ALU.add).then_inc(sum_made, 1)
                dve.wait_ge(sum_made, b + 1)
                dve.reciprocal(rinv, rowsum).then_inc(rinv_made, 1)
                dve.wait_ge(rinv_made, b + 1)
                dve.tensor_tensor(prob, expd, rinv.unsqueeze(2).broadcast_to([P, T, S]), ALU.mult).then_inc(prob_made, 1)
                dve.wait_ge(prob_made, b + 1)
                dve.tensor_copy(w_a[:, :, 0:S].bitcast(F32R), prob).then_inc(prob_hi, 1)
                dve.wait_ge(prob_hi, b + 1)
                dve.tensor_tensor(w_b[:, :, 0:S].bitcast(F32R), prob, w_a[:, :, 0:S], ALU.subtract).then_inc(prob_split, 1)

            def finish(b, t):
                dve.wait_ge(tanh_made, b * T + (t + 1))
                dve.wait_ge(attn_done, b * T + (t + 1))
                dve.scalar_tensor_tensor(prod_sb[:, t % 2, :], tanh_sb[:, t % 2, :], 1.0, attn_ps[t % 2][:, :],
                                         ALU.add, ALU.mult).then_inc(prod_made, 1)
                dve.wait_ge(prod_made, b * T + (t + 1))
                past(dve, stored[t], b * 16)
                hm = half_mask[:, bass.ds(b * T + t, 1)]
                dve.scalar_tensor_tensor(out_sb[:, t, :], prod_sb[:, t % 2, :], hm, x_rows_of[0][:, t, :],
                                         ALU.mult, ALU.add).then_inc(out_made, 1)

            x_rows_of = [None]

            def batch(b, i, more, more2):
                x_rows_of[0] = x_rows[i]
                finish(b, 0)
                if more:
                    xT_lo_tile(b + 1, 1 - i, 0)
                    xT_lo_tile(b + 1, 1 - i, 1)
                finish(b, 1)
                if more:
                    xT_lo_tile(b + 1, 1 - i, 2)
                    xT_lo_tile(b + 1, 1 - i, 3)
                if more2:
                    mt_lo(b + 2, i)
                finish(b, 2)
                if more:
                    add_sb(b + 1)
                    softmax(b + 1)
                finish(b, 3)

            for t in range(T):
                xT_lo_tile(0, 0, t)
            mt_lo(0, 0)
            mt_lo(1, 1)
            dve.wait_ge(sb_made, 2 * G)
            add_sb(0)
            softmax(0)
            for i in range(2):
                batch(i, i, True, True)
            with dve.Fori(1, B // 2 - 1) as j:
                for i in range(2):
                    batch(2 * j + i, i, True, True)
            for i in range(2):
                batch(B - 2 + i, i, i == 0, False)

        @block.gpsimd
        def _(pool):
            pool.memset(ident[:, :], 0.0).then_inc(ident_zeroed, 1)
            pool.wait_ge(ident_zeroed, 1)
            pool.affine_select(out=ident[:, :], in_=ident[:, :], compare_op=ALU.not_equal, fill=1.0, base=0,
                               pattern=[[-1, P]], channel_multiplier=1).then_inc(ident_made, 1)

            def mt_hi(b, i):
                pool.tensor_copy(mt_b[i][:, HI], mt[:, b]).then_inc(mt_split_hi, 1)

            pool.wait_ge(job_drained, J_ALL)
            mt_hi(0, 0)
            mt_hi(1, 1)

            with pool.Fori(0, B // 2 - 1) as j:
                for i in range(2):
                    pool.wait_ge(sT_done, 2 * j + (i + 1))
                    pool.nop()
                    mt_hi(2 * j + (i + 2), i)


_ARGS = ["x", "ctx_1024", "mask_BxS_ff1", "L0_xattn_Wq", "L0_xattn_bq", "L0_xattn_Wk", "L0_xattn_bk",
         "L0_xattn_Wv", "L0_xattn_bv", "L0_xattn_Wg", "L0_xattn_bg"]


def kernel(**inputs):
    import numpy as np
    import concourse.bacc as bacc
    from concourse.bass_utils import run_bass_kernel_spmd

    nc = bacc.Bacc("TRN2", target_bir_lowering=False, num_devices=1)
    arrays, args = {}, []
    for name in _ARGS:
        a = np.ascontiguousarray(inputs[name])
        arrays[f"in_{name}"] = a
        args.append(nc.dram_tensor(f"in_{name}", a.shape, mybir.dt.from_np(a.dtype), kind="ExternalInput").ap())
    out = nc.dram_tensor("out_y", (B, L, D), F32, kind="ExternalOutput").ap()
    build(nc, *args, out)
    r = run_bass_kernel_spmd(nc, [arrays], core_ids=[0])
    return r.results[0]["out_y"]
```

```python
from contextlib import ExitStack

import concourse.bass as bass
import concourse.mybir as mybir
from concourse.alu_op_type import AluOpType as ALU

F32 = mybir.dt.float32
F32R = mybir.dt.float32r
ACT = mybir.ActivationFunctionType
AX = mybir.AxisListType

P = 128
B, L, D = 16, 512, 512
S = 77
SP = S + 1
C = D // P
T = L // P
HI, LO = 0, 1
SCALE = float(D) ** -0.5

GB = 8
G = B // GB
GK = GB * SP
HB = GB // 2
QB = GB // 4
HK = HB * SP
KT = -(-GK // P)
KROWS = [min(P, GK - k * P) for k in range(KT)]

LO_A = 45
LO_B = S - LO_A
K_A, K_B = S + LO_A, S + LO_B

NBANK = 4
OTHER_KINDS = ("g_part", "ctx_in", "split", "wqbk", "bqbk", "wkbq", "diag", "bq_wg1", "ctx_bk", "sb",
               "x", "scoresT", "scores", "softmax_max", "softmax_rest")
HALF_KINDS = ("wqT", "wkT", "g", "wqg", "ctxT", "vT")
WG1, WV, WG2 = 0, 1, 2


def preparation():
    steps = []

    def add(kind, index=0, g=0, half=0):
        steps.append((kind, g, index, half))

    for c in range(C):
        add("wqT", c)
        add("wkT", c)
        if c == C - 1:
            add("vec")
        if c >= 1:
            add("g_part", c - 1)
        if c >= 2:
            for i in (2 * c - 4, 2 * c - 3):
                add("wqbk", i)
    for c in range(C):
        add("split", (WG1, c))
    add("wkbq", 0)
    for c in range(C):
        add("g", c)
        if c >= 1:
            add("wkbq", c)
    add("diag")
    for c in range(C):
        for i in (2 * c, 2 * c + 1):
            add("split", (WV, i) if i < C else (WG2, i - C))
        add("wqg", c)
        if c == 0:
            add("bq_wg1", 0)
        if 1 <= c < 3:
            add("bq_wg1", c)
        if c == 1:
            add("u")
        if c < C - 1:
            add("ctxT", c)
        if c == 1:
            add("bqbk")
        if c == C - 2:
            add("ctxT", c + 1)
            add("bq_wg1", C - 1)

    for g in range(G):
        last = g == G - 1
        for c in range(C):
            add("mt", c, g, 0)
            if (g, c) == (0, 0):
                add("btot")
            add("ctxT", c, g, 1)
            add("ctx_bk", c, g)
        rest = list(range(C))
        for k in range(KT + 1):
            if k >= 1:
                add("vT", k - 1, g)
            if last and k in (1, 2):
                add("x", 2 * k - 2)
                add("x", 2 * k - 1)
            if k == KT:
                if last:
                    add("softmax_rest")
                for c in rest:
                    add("mt", c, g, 1)
            if k < KT:
                add("v", k, g)
            if k == 0:
                for c in range(2):
                    add("mt", rest.pop(0), g, 1)
                    add("ctx_bk", C + c, g)
            if k == 1:
                for i in range(C + 2, GB):
                    add("ctx_bk", i, g)
                add("sb", 0, g)
            if last and k == 3:
                add("scoresT")
            if not last and k in (3, 4):
                add("ctxT", 2 * (k - 3), g + 1)
            if last and k == 4:
                add("scores")
                add("softmax_max")
            if k >= 1:
                add("vg", k - 1, g)
            if not last and k in (1, 2):
                add("ctx_in", 2 * k - 2, g + 1)
                add("ctx_in", 2 * k - 1, g + 1)
            if not last and k in (3, 4):
                add("ctxT", 2 * (k - 3) + 1, g + 1)
    return steps


STEPS = preparation()
JOBS = [s for s in STEPS if s[0] not in OTHER_KINDS]
JOB = {s: n for n, s in enumerate(JOBS)}
J_ALL = len(JOBS)
DRAINED = {s: n + 1 for n, s in enumerate(JOBS)}
HALVED = {s: n + 1 for n, s in enumerate(s for s in JOBS if s[0] in HALF_KINDS)}
SPLIT = {s[2]: n + 1 for n, s in enumerate(s for s in STEPS if s[0] == "split")}
DOTS = {s: n for n, s in enumerate(s for s in STEPS if s[0] in ("wqbk", "bqbk", "wkbq", "ctx_bk"))}
N_SPLIT = len(SPLIT)


def bank_of(n):
    return NBANK + n % NBANK if n <= 2 * C else (n - J_ALL) % NBANK


def last_in_bank(i):
    return max(n for n in range(2 * C, J_ALL) if bank_of(n) == i) + 1


PRODUCTS = [(HI, HI), (HI, LO), (LO, HI)]


def build(nc, x, ctx_in, mask, wq, bq, wk, bk, wv, bv, wg, bg, out):
    with ExitStack() as es:
        def sb(name, shape, dt=F32):
            return es.enter_context(nc.sbuf_tensor(name, shape, dt))

        def sem(name):
            return es.enter_context(nc.semaphore(name))

        bank = [es.enter_context(nc.psum_tensor(f"bank{i}", [P, 512], F32)) for i in range(8)]
        gate_ps, attn_ps, turn_ps = bank[0:2], bank[2:4], bank[4:6]
        score_ps, turn_a_ps = bank[6], bank[7]
        turn_b_ps = score_ps
        sT_ps = turn_a_ps

        v_dram = nc.dram_tensor("v_scratch", [B * SP, 2, 2 * D], F32, kind="Internal").ap()

        W_HL = 2 * C * D
        XT_WORDS = 2 * C * L
        SLOTS = 5
        arena_r = sb("arena_r", [P, 2 * C * GK + SLOTS * W_HL + 2 * D + 2 * 2 * D], F32R)
        at = [0]

        def take(words):
            at[0] += words
            return arena_r[:, at[0] - words:at[0]]

        def split_w(words):
            return words.rearrange("p (s c n) -> p s c n", s=2, c=C)

        ctxT_w = take(2 * C * GK)
        slot = [take(W_HL) for _ in range(SLOTS)]
        vT = take(2 * D).rearrange("p (s c k) -> p s c k", s=2, c=C)
        v_st = [w.rearrange("p (s n) -> p s n", s=2)
                for w in (take(2 * 2 * D), slot[3][:, 2 * L:2 * L + 2 * 2 * D])]
        ctxT = ctxT_w.rearrange("p (s c b k) -> p s c b k", s=2, c=C, b=GB)
        wkT, wqT, g_s, wg1_s, wg2_s = (split_w(w) for w in slot)
        wv_s = wkT
        wqg = sb("wqg", [P, 2, C, D], F32R)
        xT = [slot[1 - i][:, 0:XT_WORDS].rearrange("p (s c q) -> p s c q", s=2, c=C) for i in (0, 1)]
        v_ext = [ctxT_w[:, i * 4 * D:(i + 1) * 4 * D].rearrange("p (h n) -> p h n", h=2) for i in range(2)]
        wT = slot[3][:, 0:2 * L].rearrange("p (h q) -> p h q", h=2)
        mt_b = [sb(f"mt_b{i}", [P, 2, C, SP], F32R) for i in range(2)]

        rows_w = sb("rows_w", [P, 2, C * D])
        mt_w = sb("mt", [P, B * C * SP])
        mt = mt_w[:, :].rearrange("p (b c k) -> p b c k", b=B, c=C)
        raw_wq, raw_wk = (rows_w[:, i, :].rearrange("p (c n) -> p c n", c=C) for i in range(2))
        raw_wg1, raw_wv = (mt_w[:, i * C * D:(i + 1) * C * D].rearrange("p (c n) -> p c n", c=C) for i in range(2))
        raw_wg2 = raw_wq
        x_rows = [rows_w[:, i, :].rearrange("p (t n) -> p t n", t=T) for i in range(2)]
        work = sb("work", [P, GB * D])
        ctx_rows = work[:, :].rearrange("p (b n) -> p b n", b=GB)
        out_sb = work[:, 0:T * D].rearrange("p (t n) -> p t n", t=T)
        tanh_sb = work[:, T * D:(T + 2) * D].rearrange("p (i n) -> p i n", i=2)
        prod_sb = work[:, (T + 2) * D:(T + 4) * D].rearrange("p (i n) -> p i n", i=2)
        sb_c = sb("sb_c", [S, B])
        sT_raw = sb("sT", [P, L])
        sT = sT_raw[0:S, :]
        small = sb("small", [P, 4 * D])
        v_f, vg_f, bv_bc, btot = (small[:, i * D:(i + 1) * D] for i in range(4))
        shifted = sb("shifted", [P, T, S])[:, :, :]
        prob = shifted
        expd = sb("expd", [P, T, S])[:, :, :]
        w_a = sb("w_a", [P, T, K_A])[:, :, :]
        dot_tmp = sT_raw[:, :]
        sb_dot = sb("sb_dot", [S, GB])
        stat = sb("stat", [P, 3, T])
        rowmax, rowsum, rinv = stat[:, 0, :], stat[:, 1, :], stat[:, 2, :]
        bq_row, bk_row = v_f, vg_f
        u_row = sb("u_row", [P, D])
        w_b = u_row[:, 0:T * K_B].rearrange("p (t k) -> p t k", t=T)
        u_diag = sb("u_diag", [P, C, P])
        bq_wg1 = sb("bq_wg1", [P, D])
        u_c, wqbk_c, bqbk = sb("u_c", [P, C]), sb("wqbk_c", [P, C]), sb("bqbk", [P, 1])
        ident = sb("ident", [P, P])
        ones = sb("ones", [P, P])
        vec_rows = sb("vec_rows", [B * T + C, P])
        vec = sb("vec", [P, B * T + C])
        bq_c = vec[:, B * T:B * T + C]
        half_mask = sb("half_mask", [P, B * T])

        wq_in, wk_in = ([sem(f"{w}_in{c}") for c in range(C)] for w in ("wq", "wk"))
        wg1_in, wv_in, wg2_in = sem("wg1_in"), sem("wv_in"), sem("wg2_in")
        vec_in, brow_in, ctx_in_s = sem("vec_in"), sem("brow_in"), [sem(f"ctx_in_s{h}") for h in range(2)]
        dots_made, sb_made = sem("dots_made"), sem("sb_made")
        ones_made, ident_zeroed, ident_made = sem("ones_made"), sem("ident_zeroed"), sem("ident_made")
        vec_made, pads_made = sem("vec_made"), sem("pads_made")
        diag_made, bq_wg1_made = sem("diag_made"), sem("bq_wg1_made")
        job_done = sem("job_done")
        hi_made = sem("hi_made")
        job_drained = sem("job_drained")
        w_hi, w_split = sem("w_hi"), sem("w_split")
        v_hi, v_lo, vg_hi, vg_lo = sem("v_hi"), sem("v_lo"), sem("vg_hi"), sem("vg_lo")
        bg_in, bv_in = sem("bg_in"), sem("bv_in")
        v_stored, vg_stored = ([sem(f"{v}_stored{i}") for i in range(2)] for v in ("v", "vg"))
        x_in = [[sem(f"x_in{i}{t}") for t in range(T)] for i in range(2)]
        vext_in = [sem(f"vext_in{i}") for i in range(2)]
        vext_made = sem("vext_made")
        mt_split_hi, mt_split = sem("mt_split_hi"), sem("mt_split")
        x_turned, xT_hi, xT_made = sem("x_turned"), sem("xT_hi"), sem("xT_made")
        sT_done, sT_made, scores_done = sem("sT_done"), sem("sT_made"), sem("scores_done")
        max_made, shift_made, exp_made = sem("max_made"), sem("shift_made"), sem("exp_made")
        sum_made, rinv_made, prob_made = sem("sum_made"), sem("rinv_made"), sem("prob_made")
        prob_hi, prob_split = sem("prob_hi"), sem("prob_split")
        prob_stacked_a, prob_stacked_b = sem("prob_stacked_a"), sem("prob_stacked_b")
        wa_turned, wb_turned, wTa_made, wTb_made = sem("wa_turned"), sem("wb_turned"), sem("wTa_made"), sem("wTb_made")
        gate_done, attn_done = sem("gate_done"), sem("attn_done")
        tanh_made, prod_made, out_made = sem("tanh_made"), sem("prod_made"), sem("out_made")
        stored = [sem(f"stored{t}") for t in range(T)]

        x_v = x.rearrange("b (t p) d -> b t p d", p=P)
        out_v = out.rearrange("b (t p) d -> b t p d", p=P)

        def w_rows(w):
            return w.rearrange("(c p) n -> p c n", p=P)

        def f32(ap):
            return ap.bitcast(F32)

        def past(eng, sem_, value):
            if not isinstance(value, int) or value > 0:
                eng.wait_ge(sem_, value)

        block = es.enter_context(nc.Block())

        @block.sync
        def _(sync):
            for c in range(C):
                for raw, w, landed in ((raw_wq, wq, wq_in), (raw_wk, wk, wk_in)):
                    cols = slice(c * P, (c + 1) * P)
                    sync.dma_start(raw[:, :, cols], w_rows(w[:, cols])).then_inc(landed[c], 16)
            sync.dma_start(vec_rows[0:B * T, :], mask.rearrange("b (t p) -> (b t) p", p=P)).then_inc(vec_in, 16)
            sync.dma_start(vec_rows[B * T:B * T + C, :], bq.rearrange("(c p) -> c p", p=P)).then_inc(vec_in, 16)
            for row, b_ in ((bq_row, bq), (bk_row, bk)):
                sync.dma_start(row, b_.rearrange("(a n) -> a n", a=1).broadcast_to([P, D])).then_inc(brow_in, 16)
            sync.dma_start(raw_wg1, w_rows(wg[0:D, :])).then_inc(wg1_in, 16)
            sync.dma_start(raw_wv, w_rows(wv)).then_inc(wv_in, 16)
            for row, b_, landed in ((btot, bg, bg_in), (bv_bc, bv, bv_in)):
                sync.dma_start(row, b_.rearrange("(a n) -> a n", a=1).broadcast_to([P, D])).then_inc(landed, 16)

            def load_ctx(g, q):
                b0 = g * GB + q * QB
                sync.dma_start(ctx_rows[0:S, q * QB:(q + 1) * QB],
                               ctx_in[b0:b0 + QB].rearrange("b k d -> k b d")).then_inc(ctx_in_s[q // 2], 16)

            for q in range(4):
                load_ctx(0, q)
            sync.wait_ge(job_done, DRAINED["wqT", 0, C - 1, 0])
            sync.wait_ge(dots_made, DOTS["wqbk", 0, C - 1, 0] + 1)
            sync.dma_start(raw_wg2, w_rows(wg[D:2 * D, :])).then_inc(wg2_in, 16)

            def load_vext(b, i):
                r = b * SP
                sync.dma_start(f32(v_ext[i][0:S, 0, :]), v_dram[bass.ds(r, S), HI, :]).then_inc(vext_in[i], 16)
                sync.dma_start(f32(v_ext[i][S:K_A, 0, :]), v_dram[bass.ds(r, LO_A), LO, :]).then_inc(vext_in[i], 16)
                sync.dma_start(f32(v_ext[i][S:K_B, 1, :]), v_dram[bass.ds(r + LO_A, LO_B), LO, :]).then_inc(vext_in[i], 16)

            def wait_stored(tiles):
                for i in range(2):
                    for done in (v_stored, vg_stored):
                        sync.wait_ge(done[i], 16 * ((tiles + 1 - i) // 2))

            for step in STEPS:
                kind, g, k, _ = step
                if kind in ("v", "vg"):
                    if kind == "vg" and (g, k) == (G - 1, KT - 1):
                        wait_stored(KT)
                        sync.wait_ge(job_done, DRAINED["mt", G - 1, C - 1, 1])
                        for b in range(2):
                            load_vext(b, b)
                    n = g * KT + k
                    made, done, cols = (v_lo, v_stored, 0) if kind == "v" else (vg_lo, vg_stored, D)
                    r0 = g * GK + k * P
                    sync.wait_ge(made, n + 1)
                    sync.dma_start(v_dram[r0:r0 + KROWS[k], :, cols:cols + D],
                                   f32(v_st[n % 2][0:KROWS[k], :, cols:cols + D])).then_inc(done[n % 2], 16)
                if step == ("mt", G - 1, 0, 0):
                    sync.wait_ge(w_split, N_SPLIT)
                    sync.wait_ge(dots_made, DOTS["wkbq", 0, C - 1, 0] + 1)
                    for b in range(2):
                        for t in range(T):
                            sync.dma_start(x_rows[b][:, t, :], x_v[b, t]).then_inc(x_in[b][t], 16)
                if kind == "ctx_in":
                    sync.wait_ge(job_done, DRAINED["ctxT", g - 1, C - 1, 1])
                    sync.wait_ge(dots_made, DOTS["ctx_bk", g - 1, GB - 1, 0] + 1)
                    load_ctx(g, k)
            wait_stored(G * KT)

            def batch(b, i, more):
                for t in range(T):
                    sync.wait_ge(out_made, b * T + (t + 1))
                    sync.dma_start(out_v[b, t], out_sb[:, t, :]).then_inc(stored[t], 16)
                    if more:
                        sync.dma_start(x_rows[i][:, t, :], x_v[b + 2, t]).then_inc(x_in[i][t], 16)
                if more:
                    sync.wait_ge(attn_done, b * T + T)
                    load_vext(b + 2, i)

            for i in range(2):
                batch(i, i, True)
            with sync.Fori(1, B // 2 - 1) as j:
                for i in range(2):
                    batch(2 * j + i, i, True)
            for i in range(2):
                batch(B - 2 + i, i, False)
            for t in range(T):
                sync.wait_ge(stored[t], 16 * B)

        @block.tensor
        def _(pe):
            def products(ps, lhs, rhs, done, made=None, value=None, chunks=range(C)):
                for c in chunks:
                    if made is not None:
                        pe.wait_ge(made, value(c))
                    for n, (s, m) in enumerate(PRODUCTS):
                        last = pe.matmul(ps, lhs(s, c), rhs(m, c), start=(c == 0 and n == 0), stop=(c == C - 1 and n == 2))
                if c == C - 1:
                    last.then_inc(done, 1)

            def turn_x(i, t):
                for c in range(C):
                    last = pe.transpose(turn_ps[t % 2][:, c * P:(c + 1) * P], x_rows[i][:, t, c * P:(c + 1) * P], ident[:, :])
                last.then_inc(x_turned, 1)

            def scores_T(b, i):
                pe.wait_ge(xT_made, b * T + T)
                pe.wait_ge(mt_split, b + 1)
                products(sT_ps[0:S, :], lambda s, c: mt_b[i][:, s, c, 0:S], lambda s, c: xT[i][:, s, c, :], sT_done)

            def turn_scores(b):
                pe.wait_ge(sT_made, b + 1)
                for t in range(T):
                    last = pe.transpose(score_ps[:, t * S:(t + 1) * S], sT[:, t * P:(t + 1) * P], ident[0:S, 0:S])
                last.then_inc(scores_done, 1)

            def gate_main(i, t, chunks):
                q = slice(t * P, (t + 1) * P)
                for c in chunks:
                    for s, m in PRODUCTS:
                        pe.matmul(gate_ps[t % 2][:, :], xT[i][:, s, c, q], wqg[:, m, c, :],
                                  start=(c == 0 and (s, m) == PRODUCTS[0]), stop=False)

            def turn_probs(b):
                pe.wait_ge(prob_split, b + 1)
                pe.wait_ge(prob_stacked_a, b + 1)
                pe.wait_ge(prob_stacked_b, b + 1)
                for t in range(T):
                    last = pe.transpose(turn_a_ps[0:K_A, t * P:(t + 1) * P], w_a[:, t, :], ident[:, :])
                last.then_inc(wa_turned, 1)
                for t in range(T):
                    last = pe.transpose(turn_b_ps[0:K_B, t * P:(t + 1) * P], w_b[:, t, :], ident[:, :])
                last.then_inc(wb_turned, 1)

            def attend(b, i, t):
                q = slice(t * P, (t + 1) * P)
                for ps, cols, done in ((gate_ps[t % 2], slice(D, 2 * D), gate_done), (attn_ps[t % 2], slice(0, D), attn_done)):
                    first = done is attn_done
                    pe.matmul(ps[:, :], wT[0:K_A, 0, q], v_ext[i][0:K_A, 0, cols], start=first, stop=False)
                    pe.matmul(ps[:, :], wT[0:K_B, 1, q], v_ext[i][0:K_B, 1, cols], start=False, stop=True).then_inc(done, 1)

            def batch(b, half, i, more):
                n = 1 - i
                first = isinstance(b, int) and b == 0
                gate_main(i, 0, range(C))
                if first:
                    pe.wait_ge(job_drained, J_ALL)
                else:
                    pe.wait_ge(tanh_made, b * T)
                gate_main(i, 1, range(C // 2))
                turn_probs(b)
                gate_main(i, 1, range(C // 2, C))
                pe.wait_ge(wTa_made, b + 1)
                pe.wait_ge(wTb_made, b + 1)
                pe.wait_ge(vext_made, b + 1)
                attend(b, i, 0)

                def turn_next(t):
                    if more:
                        pe.wait_ge(x_in[n][t], (half + i) * 16 + 16)
                        pe.wait_ge(xT_made, b * T + (T + t - 1))
                        turn_x(n, t)

                turn_next(0)
                turn_next(1)
                past(pe, prod_made, b * T)
                attend(b, i, 1)
                pe.wait_ge(tanh_made, b * T + 1)
                gate_main(i, 2, range(C // 2))
                turn_next(2)
                turn_next(3)
                gate_main(i, 2, range(C // 2, C))
                pe.wait_ge(prod_made, b * T + 1)
                attend(b, i, 2)
                if more:
                    scores_T(b + 1, n)
                pe.wait_ge(tanh_made, b * T + 2)
                gate_main(i, 3, range(C))
                if more:
                    turn_scores(b + 1)
                pe.wait_ge(prod_made, b * T + 2)
                attend(b, i, 3)
                if more:
                    pe.wait_ge(tanh_made, b * T + 3)
                    pe.wait_ge(prod_made, b * T + 3)

            def g_product(cc, c):
                products(bank[bank_of(JOB["g", 0, cc, 0])][:, :], lambda s, c: wkT[:, s, c, cc * P:(cc + 1) * P],
                         lambda s, c: wqT[:, s, c, :], job_done,
                         job_drained, lambda c: DRAINED["wkT", 0, c, 0], (c,))

            pe.wait_ge(ident_made, 1)
            pe.wait_ge(ones_made, 1)
            NV = B * T + C
            ctx_keys = ctxT_w.rearrange("p (s c k) -> p s c k", s=2, c=C)
            for step in STEPS:
                kind, g, k, h = step
                hs = slice(h * HB, (h + 1) * HB)
                if step in JOB:
                    ps = bank[bank_of(JOB[step])]
                    if JOB[step] >= NBANK:
                        pe.wait_ge(job_drained, JOB[step] - NBANK + 1)
                if kind in ("wqT", "wkT"):
                    raw, landed = (raw_wq, wq_in) if kind == "wqT" else (raw_wk, wk_in)
                    pe.wait_ge(landed[k], 16)
                    for rc in range(C):
                        last = pe.transpose(ps[:, rc * P:(rc + 1) * P], raw[:, rc, k * P:(k + 1) * P], ident[:, :])
                    last.then_inc(job_done, 1)
                elif kind == "vec":
                    pe.wait_ge(vec_in, 32)
                    pe.transpose(ps[:, 0:NV], vec_rows[:, :], ident[0:NV, 0:NV]).then_inc(job_done, 1)
                elif kind == "g_part":
                    for cc in range(C):
                        g_product(cc, k)
                elif kind == "g":
                    g_product(k, C - 1)
                elif kind == "u":
                    pe.wait_ge(diag_made, 1)
                    pe.matmul(ps[:, :], ones[:, :], u_diag[:, :, :].rearrange("p c k -> p (c k)"), start=True, stop=True).then_inc(job_done, 1)
                elif kind == "btot":
                    pe.wait_ge(bq_wg1_made, C)
                    pe.matmul(ps[:, :], ones[:, :], bq_wg1[:, :], start=True, stop=True).then_inc(job_done, 1)
                elif kind == "wqg":
                    products(ps[:, :], lambda s, c: wqT[:, s, c, k * P:(k + 1) * P], lambda s, c: wg1_s[:, s, c, :], job_done,
                             w_split, lambda c: SPLIT[WG1, c])
                elif kind == "ctxT":
                    pe.wait_ge(ctx_in_s[h], g * 32 + 32)
                    for i in range(HB):
                        last = pe.transpose(ps[:, i * SP:i * SP + S], ctx_rows[0:S, h * HB + i, k * P:(k + 1) * P], ident[0:S, 0:S])
                    last.then_inc(job_done, 1)
                elif kind == "mt":
                    products(ps[:, 0:HK], lambda s, c: g_s[:, s, c, k * P:(k + 1) * P], lambda s, c: ctxT[:, s, c, hs, :], job_done,
                             job_drained, lambda c: DRAINED["ctxT", g, c, h])
                elif kind == "v":
                    n = KROWS[k]
                    pe.wait_ge(w_split, SPLIT[WV, C - 1])
                    products(ps[0:n, :], lambda s, c: ctx_keys[:, s, c, k * P:k * P + n], lambda s, c: wv_s[:, s, c, :], job_done)
                elif kind == "vT":
                    n = KROWS[k]
                    pe.wait_ge(job_drained, DRAINED["v", g, k, 0])
                    for c in range(C):
                        last = pe.transpose(ps[:, c * P:c * P + n], v_f[0:n, c * P:(c + 1) * P], ident[0:n, 0:n])
                    last.then_inc(job_done, 1)
                elif kind == "vg":
                    n = KROWS[k]
                    pe.wait_ge(w_split, SPLIT[WG2, C - 1])
                    pe.wait_ge(job_drained, DRAINED["vT", g, k, 0])
                    products(ps[0:n, :], lambda s, c: vT[:, s, c, 0:n], lambda s, c: wg2_s[:, s, c, :], job_done)
                elif kind == "x":
                    pe.wait_ge(x_in[0][k], 16)
                    if k >= 2:
                        pe.wait_ge(xT_made, k - 1)
                    turn_x(0, k)
                elif kind == "scoresT":
                    scores_T(0, 0)
                elif kind == "scores":
                    turn_scores(0)

            pe.wait_ge(job_drained, last_in_bank(0))
            for i in range(2):
                batch(i, 0, i, True)
            with pe.Fori(1, B // 2 - 1) as j:
                for i in range(2):
                    batch(2 * j + i, j, i, True)
            for i in range(2):
                batch(B - 2 + i, B // 2 - 1, i, i == 0)

        @block.scalar
        def _(act):
            def xT_hi_tile(b, i, t):
                act.wait_ge(x_turned, b * T + (t + 1))
                act.activation(xT[i][:, HI, :, t * P:(t + 1) * P], turn_ps[t % 2][:, :].rearrange("p (c q) -> p c q", c=C),
                               ACT.Copy).then_inc(xT_hi, 1)

            def stack_probs(b):
                act.wait_ge(prob_hi, b + 1)
                act.activation(w_a[:, :, S:K_A], w_a[:, :, 0:LO_A], ACT.Copy).then_inc(prob_stacked_a, 1)
                act.activation(w_b[:, :, S:K_B], w_a[:, :, LO_A:S], ACT.Copy).then_inc(prob_stacked_b, 1)

            def exps(b):
                act.wait_ge(shift_made, b + 1)
                act.activation(expd, shifted, ACT.Exp, scale=SCALE).then_inc(exp_made, 1)

            def tanh_tile(b, t):
                act.wait_ge(gate_done, b * T + (t + 1))
                act.activation(tanh_sb[:, t % 2, :], gate_ps[t % 2][:, :], ACT.Tanh, scale=0.5).then_inc(tanh_made, 1)

            def copy_v_hi(i, loads):
                act.wait_ge(vext_in[i], 3 * 16 * loads)
                act.activation(v_ext[i][0:S, 1, :], f32(v_ext[i][0:S, 0, :]), ACT.Copy).then_inc(vext_made, 1)

            def batch(b, half, i, more):
                act.wait_ge(wa_turned, b + 1)
                act.activation(wT[0:K_A, 0, :], turn_a_ps[0:K_A, :], ACT.Copy).then_inc(wTa_made, 1)
                act.wait_ge(wb_turned, b + 1)
                act.activation(wT[0:K_B, 1, :], turn_b_ps[0:K_B, :], ACT.Copy).then_inc(wTb_made, 1)
                tanh_tile(b, 0)
                if more:
                    xT_hi_tile(b + 1, 1 - i, 0)
                    xT_hi_tile(b + 1, 1 - i, 1)
                past(act, prod_made, b * T)
                tanh_tile(b, 1)
                if more:
                    xT_hi_tile(b + 1, 1 - i, 2)
                    xT_hi_tile(b + 1, 1 - i, 3)
                act.wait_ge(prod_made, b * T + 1)
                tanh_tile(b, 2)
                if more:
                    copy_v_hi(1 - i, half + (1 + i))
                act.wait_ge(prod_made, b * T + 2)
                tanh_tile(b, 3)
                if more:
                    exps(b + 1)
                    stack_probs(b + 1)
                if more:
                    act.wait_ge(prod_made, b * T + 3)

            def hi_of(ps, dst):
                act.wait_ge(job_done, DRAINED[step])
                act.activation(dst, ps, ACT.Copy).then_inc(hi_made, 1)

            for step in STEPS:
                kind, g, k, h = step
                if step in JOB:
                    ps = bank[bank_of(JOB[step])]
                if kind in ("wqT", "wkT", "g", "wqg"):
                    dst = {"wqT": wqT, "wkT": wkT, "g": g_s, "wqg": wqg}[kind]
                    hi_of(ps[:, :], dst[:, HI, k, :])
                elif kind == "split":
                    w, c = k
                    raw, dst, landed = ((raw_wg1, wg1_s, wg1_in), (raw_wv, wv_s, wv_in), (raw_wg2, wg2_s, wg2_in))[w]
                    if c == 0:
                        act.wait_ge(landed, 16)
                    if k == (WV, 0):
                        act.wait_ge(job_done, DRAINED["g", 0, C - 1, 0])
                    act.activation(dst[:, HI, c, :], raw[:, c, :], ACT.Copy).then_inc(w_hi, 1)
                elif kind == "ctxT":
                    if (g, k, h) == (0, 0, 0):
                        act.wait_ge(pads_made, 1)
                    ps = ps[:, 0:HK].rearrange("p (b k) -> p b k", b=HB)
                    hi_of(ps[:, :, 0:S], ctxT[:, HI, k, h * HB:(h + 1) * HB, 0:S])
                elif kind == "vT":
                    n = KROWS[k]
                    ps = ps[:, :].rearrange("p (c k) -> p c k", c=C)
                    hi_of(ps[:, :, 0:n], vT[:, HI, :, 0:n])
                elif kind in ("v", "vg"):
                    src, done, stored_, cols = (v_f, v_hi, v_stored, 0) if kind == "v" else (vg_f, vg_hi, vg_stored, D)
                    n, i = KROWS[k], g * KT + k
                    act.wait_ge(job_drained, DRAINED[step])
                    if i >= 2:
                        act.wait_ge(stored_[i % 2], 16 * (i // 2))
                    act.activation(v_st[i % 2][0:n, HI, cols:cols + D], src[0:n, :], ACT.Copy).then_inc(done, 1)
                elif kind == "x":
                    xT_hi_tile(0, 0, k)
                elif kind == "softmax_max":
                    exps(0)
                elif kind == "softmax_rest":
                    stack_probs(0)

            copy_v_hi(0, 1)
            for i in range(2):
                batch(i, 0, i, True)
            with act.Fori(1, B // 2 - 1) as j:
                for i in range(2):
                    batch(2 * j + i, j, i, True)
            for i in range(2):
                batch(B - 2 + i, B // 2 - 1, i, i == 0)

        @block.vector
        def _(dve):
            dve.memset(ones[:, :], 1.0).then_inc(ones_made, 1)
            dve.memset(f32(ctxT[:, :, :, :, S:SP].rearrange("p s c b k -> p (s c b) k")), 0.0).then_inc(pads_made, 1)

            def mt_lo(b, i):
                dve.wait_ge(mt_split_hi, b + 1)
                dve.tensor_tensor(mt_b[i][:, LO], mt[:, b], f32(mt_b[i][:, HI]), ALU.subtract).then_inc(mt_split, 1)

            def xT_lo_tile(b, i, t):
                dve.wait_ge(xT_hi, b * T + (t + 1))
                q = slice(t * P, (t + 1) * P)
                dve.tensor_tensor(xT[i][:, LO, :, q], turn_ps[t % 2][:, :].rearrange("p (c q) -> p c q", c=C),
                                  f32(xT[i][:, HI, :, q]), ALU.subtract).then_inc(xT_made, 1)

            def add_sb(b):
                dve.wait_ge(sT_done, b + 1)
                dve.tensor_scalar(sT, sT_ps[0:S, :], sb_c[0:S, bass.ds(b, 1)], None, ALU.add).then_inc(sT_made, 1)

            def softmax_max(b):
                sc = score_ps[:, 0:T * S].rearrange("p (t k) -> p t k", t=T)
                dve.wait_ge(scores_done, b + 1)
                dve.tensor_reduce(rowmax, sc, AX.X, ALU.max).then_inc(max_made, 1)
                dve.wait_ge(max_made, b + 1)
                dve.tensor_tensor(shifted, sc, rowmax.unsqueeze(2).broadcast_to([P, T, S]), ALU.subtract).then_inc(shift_made, 1)

            def softmax_rest(b):
                dve.wait_ge(exp_made, b + 1)
                dve.tensor_reduce(rowsum, expd, AX.X, ALU.add).then_inc(sum_made, 1)
                dve.wait_ge(sum_made, b + 1)
                dve.reciprocal(rinv, rowsum).then_inc(rinv_made, 1)
                dve.wait_ge(rinv_made, b + 1)
                dve.tensor_tensor(prob, expd, rinv.unsqueeze(2).broadcast_to([P, T, S]), ALU.mult).then_inc(prob_made, 1)
                dve.wait_ge(prob_made, b + 1)
                dve.tensor_copy(w_a[:, :, 0:S].bitcast(F32R), prob).then_inc(prob_hi, 1)
                dve.wait_ge(prob_hi, b + 1)
                dve.tensor_tensor(w_b[:, :, 0:S].bitcast(F32R), prob, w_a[:, :, 0:S], ALU.subtract).then_inc(prob_split, 1)

            def product(b, t):
                dve.wait_ge(tanh_made, b * T + (t + 1))
                dve.wait_ge(attn_done, b * T + (t + 1))
                if t >= 2:
                    dve.wait_ge(out_made, b * T + (t - 1))
                else:
                    past(dve, out_made, b * T + (t - 1))
                dve.scalar_tensor_tensor(prod_sb[:, t % 2, :], tanh_sb[:, t % 2, :], 1.0, attn_ps[t % 2][:, :],
                                         ALU.add, ALU.mult).then_inc(prod_made, 1)

            def output(b, i, t):
                dve.wait_ge(prod_made, b * T + (t + 1))
                past(dve, stored[t], b * 16)
                dve.scalar_tensor_tensor(out_sb[:, t, :], prod_sb[:, t % 2, :], half_mask[:, bass.ds(b * T + t, 1)],
                                         x_rows[i][:, t, :], ALU.mult, ALU.add).then_inc(out_made, 1)

            def batch(b, i, more, more2):
                n = 1 - i
                product(b, 0)
                if more:
                    xT_lo_tile(b + 1, n, 0)
                    xT_lo_tile(b + 1, n, 1)
                output(b, i, 0)
                product(b, 1)
                if more:
                    xT_lo_tile(b + 1, n, 2)
                    xT_lo_tile(b + 1, n, 3)
                output(b, i, 1)
                if more2:
                    mt_lo(b + 2, i)
                product(b, 2)
                output(b, i, 2)
                if more:
                    add_sb(b + 1)
                    softmax_max(b + 1)
                    softmax_rest(b + 1)
                product(b, 3)
                output(b, i, 3)

            def lo_of(ps, dst_hi, dst_lo):
                dve.wait_ge(hi_made, HALVED[step])
                dve.tensor_tensor(dst_lo, ps, f32(dst_hi), ALU.subtract).then_inc(job_drained, 1)

            def dot(rows, row, col):
                if DOTS[step]:
                    dve.wait_ge(dots_made, DOTS[step])
                dve.tensor_tensor_reduce(dot_tmp[0:rows.shape[0]], rows, row, 1.0, 0.0, ALU.mult, ALU.add, col).then_inc(dots_made, 1)

            def stage_lo(kind, g, k):
                src, hi, lo, cols = (v_f, v_hi, v_lo, 0) if kind == "v" else (vg_f, vg_hi, vg_lo, D)
                n, i = KROWS[k], g * KT + k
                dve.wait_ge(hi, i + 1)
                dve.tensor_tensor(v_st[i % 2][0:n, LO, cols:cols + D], src[0:n, :], f32(v_st[i % 2][0:n, HI, cols:cols + D]),
                                  ALU.subtract).then_inc(lo, 1)

            for step in STEPS:
                kind, g, k, h = step
                if step in JOB:
                    ps = bank[bank_of(JOB[step])]
                    ps_b = ps[:, 0:HK].rearrange("p (b k) -> p b k", b=HB)
                if kind in ("wqT", "wkT", "g", "wqg"):
                    dst = {"wqT": wqT, "wkT": wkT, "g": g_s, "wqg": wqg}[kind]
                    lo_of(ps[:, :], dst[:, HI, k, :], dst[:, LO, k, :])
                elif kind == "vec":
                    dve.wait_ge(job_done, DRAINED[step])
                    dve.tensor_copy(vec[:, :], ps[:, 0:B * T + C]).then_inc(vec_made, 1)
                    dve.wait_ge(vec_made, 1)
                    dve.tensor_scalar(half_mask[:, :], vec[:, 0:B * T], 0.5, None, ALU.mult).then_inc(job_drained, 1)
                elif kind == "wqbk":
                    dve.wait_ge(brow_in, 32)
                    dve.wait_ge(wq_in[C - 1], 16)
                    dot(raw_wq[:, k, :], bk_row, wqbk_c[:, k:k + 1])
                elif kind == "bqbk":
                    dot(bq_row, bk_row, bqbk[:, 0:1])
                elif kind == "wkbq":
                    dve.wait_ge(wk_in[C - 1], 16)
                    dot(raw_wk[:, k, :], bq_row, u_c[:, k:k + 1])
                elif kind == "diag":
                    dve.wait_ge(dots_made, DOTS["wkbq", 0, C - 1, 0] + 1)
                    dve.wait_ge(ident_made, 1)
                    dve.tensor_tensor(u_diag[:, :, :], ident[:, :].unsqueeze(1).broadcast_to([P, C, P]),
                                      u_c[:, :].unsqueeze(2).broadcast_to([P, C, P]), ALU.mult).then_inc(diag_made, 1)
                elif kind == "bq_wg1":
                    if k == 0:
                        dve.wait_ge(wg1_in, 16)
                        dve.tensor_scalar(bq_wg1[:, :], raw_wg1[:, 0, :], bq_c[:, 0:1], None, ALU.mult).then_inc(bq_wg1_made, 1)
                    else:
                        dve.wait_ge(bq_wg1_made, k)
                        dve.scalar_tensor_tensor(bq_wg1[:, :], raw_wg1[:, k, :], bq_c[:, k:k + 1], bq_wg1[:, :],
                                                 ALU.mult, ALU.add).then_inc(bq_wg1_made, 1)
                elif kind == "u":
                    dve.wait_ge(job_done, DRAINED[step])
                    dve.tensor_copy(u_row[:, :], ps[:, :]).then_inc(job_drained, 1)
                elif kind == "btot":
                    dve.wait_ge(bg_in, 16)
                    dve.wait_ge(job_done, DRAINED[step])
                    dve.tensor_tensor(btot, ps[:, :], btot, ALU.add).then_inc(job_drained, 1)
                elif kind == "ctxT":
                    bs = slice(h * HB, (h + 1) * HB)
                    lo_of(ps_b[:, :, 0:S], ctxT[:, HI, k, bs, 0:S], ctxT[:, LO, k, bs, 0:S])
                elif kind == "ctx_bk":
                    dve.wait_ge(ctx_in_s[k // HB], g * 32 + 32)
                    if (g, k) == (0, 0):
                        dve.wait_ge(job_drained, DRAINED["u", 0, 0, 0])
                    dot(ctx_rows[0:S, k, :], u_row[0:S, :], sb_dot[:, k:k + 1])
                elif kind == "sb":
                    dve.wait_ge(dots_made, DOTS["ctx_bk", g, GB - 1, 0] + 1)
                    dve.tensor_scalar(sb_c[:, g * GB:(g + 1) * GB], sb_dot[:, :], bqbk[0:S, 0:1], None, ALU.add).then_inc(sb_made, 1)
                    dve.wait_ge(sb_made, g + 1)
                elif kind == "mt":
                    if (g, k, h) == (0, 0, 0):
                        dve.wait_ge(w_split, N_SPLIT)
                        dve.wait_ge(bq_wg1_made, C)
                    dve.wait_ge(job_done, DRAINED[step])
                    b0 = g * GB + h * HB
                    dve.tensor_scalar(mt[:, b0:b0 + HB, k, :], ps_b, wqbk_c[:, k:k + 1], None, ALU.add).then_inc(job_drained, 1)
                elif kind == "vT":
                    n = KROWS[k]
                    ps_c = ps[:, :].rearrange("p (c k) -> p c k", c=C)
                    lo_of(ps_c[:, :, 0:n], vT[:, HI, :, 0:n], vT[:, LO, :, 0:n])
                elif kind in ("v", "vg"):
                    n = KROWS[k]
                    dst, bias, read = (v_f, bv_bc, v_lo) if kind == "v" else (vg_f, btot, vg_lo)
                    if g * KT + k:
                        dve.wait_ge(read, g * KT + k)
                    elif kind == "v":
                        dve.wait_ge(bv_in, 16)
                    dve.wait_ge(job_done, DRAINED[step])
                    dve.tensor_tensor(dst[0:n, :], ps[0:n, :], bias[0:n, :], ALU.add).then_inc(job_drained, 1)
                    if kind == "vg":
                        if k + 1 < KT:
                            stage_lo("v", g, k + 1)
                        stage_lo("vg", g, k)
                    elif k == 0:
                        stage_lo("v", g, 0)
                elif kind == "x":
                    xT_lo_tile(0, 0, k)
                    if k < 2:
                        mt_lo(k, k)
                elif kind == "scoresT":
                    add_sb(0)
                elif kind == "softmax_max":
                    softmax_max(0)
                elif kind == "softmax_rest":
                    softmax_rest(0)

            for i in range(2):
                batch(i, i, True, True)
            with dve.Fori(1, B // 2 - 1) as j:
                for i in range(2):
                    batch(2 * j + i, i, True, True)
            for i in range(2):
                batch(B - 2 + i, i, i == 0, False)

        @block.gpsimd
        def _(pool):
            pool.memset(ident[:, :], 0.0).then_inc(ident_zeroed, 1)
            pool.wait_ge(ident_zeroed, 1)
            pool.affine_select(out=ident[:, :], in_=ident[:, :], compare_op=ALU.not_equal, fill=1.0, base=0,
                               pattern=[[-1, P]], channel_multiplier=1).then_inc(ident_made, 1)

            def mt_hi(b, i):
                pool.tensor_copy(mt_b[i][:, HI], mt[:, b]).then_inc(mt_split_hi, 1)

            for step in STEPS:
                if step[0] == "split":
                    w, c = step[2]
                    raw, dst = ((raw_wg1, wg1_s), (raw_wv, wv_s), (raw_wg2, wg2_s))[w]
                    pool.wait_ge(w_hi, SPLIT[w, c])
                    pool.tensor_tensor(dst[:, LO, c, :], raw[:, c, :], f32(dst[:, HI, c, :]), ALU.subtract).then_inc(w_split, 1)

            pool.wait_ge(job_drained, DRAINED["mt", 0, C - 1, 1])
            mt_hi(0, 0)
            mt_hi(1, 1)

            with pool.Fori(0, B // 2 - 1) as j:
                for i in range(2):
                    pool.wait_ge(sT_done, 2 * j + (i + 1))
                    pool.nop()
                    mt_hi(2 * j + (i + 2), i)


_ARGS = ["x", "ctx_1024", "mask_BxS_ff1", "L0_xattn_Wq", "L0_xattn_bq", "L0_xattn_Wk", "L0_xattn_bk",
         "L0_xattn_Wv", "L0_xattn_bv", "L0_xattn_Wg", "L0_xattn_bg"]


def kernel(**inputs):
    import numpy as np
    import concourse.bacc as bacc
    from concourse.bass_utils import run_bass_kernel_spmd

    nc = bacc.Bacc("TRN2", target_bir_lowering=False, num_devices=1)
    arrays, args = {}, []
    for name in _ARGS:
        a = np.ascontiguousarray(inputs[name])
        arrays[f"in_{name}"] = a
        args.append(nc.dram_tensor(f"in_{name}", a.shape, mybir.dt.from_np(a.dtype), kind="ExternalInput").ap())
    out = nc.dram_tensor("out_y", (B, L, D), F32, kind="ExternalOutput").ap()
    build(nc, *args, out)
    r = run_bass_kernel_spmd(nc, [arrays], core_ids=[0])
    return r.results[0]["out_y"]
```
